# Optimizing a Trainium2 kernel written in Bass

```python
import numpy as np
import jax
import jax.numpy as jnp

def _softmax(x, axis=-1):
    return jax.nn.softmax(x, axis=axis)

def _gelu(x):
    return jax.nn.gelu(x, approximate=True)

def _silu(x):
    return jax.nn.silu(x)

def _sigmoid(x):
    return jax.nn.sigmoid(x)

def _layernorm(x, axis=-1, eps=1e-05):
    m = jnp.mean(x, axis=axis, keepdims=True)
    v = jnp.var(x, axis=axis, keepdims=True)
    return (x - m) / jnp.sqrt(v + eps)

def _scatter_add(tgt, idx, src, axis=0):
    return tgt.at[idx].add(src)

def _segment_sum(src, seg, n):
    return jax.ops.segment_sum(src, seg, n)
kernel_name = 'mk_cond_seq_d1_seqx_r2_9059db'

def setup_inputs(seed: int=0):
    np.random.seed(seed)
    _w = jnp.asarray

    def _rec_inputs():
        import jax
        import jax.numpy as jnp
        _rk = jax.random.key(seed)
        x = 7.22e-05 + 1 * jax.random.normal(jax.random.fold_in(_rk, 1), (2, 2048, 512), jnp.float32)
        _lenS = 2048 - jax.random.randint(jax.random.fold_in(_rk, 7), (2,), 0, max(1, 2048 // 4) + 1, jnp.int32)
        _lenS2 = 2048 - jax.random.randint(jax.random.fold_in(_rk, 8), (2,), 0, max(1, 2048 // 4) + 1, jnp.int32)
        cond_2048 = 0.00782532 + 1.00527 * jax.random.normal(jax.random.fold_in(_rk, 11), (2, 1024), jnp.float32)
        _validS = jnp.arange(2048)[None, :] < _lenS[:, None]
        _validS2 = jnp.arange(2048)[None, :] < _lenS2[:, None]
        _causal = jnp.tril(jnp.ones((2048, 2048), dtype=bool))
        mask_BxSx1_fk1 = jnp.where(jnp.ones((2, 2048, 1), dtype=bool), 1.0, 0.0).astype(jnp.float32)
        return (x, cond_2048, mask_BxSx1_fk1)
    x, cond_2048, mask_BxSx1_fk1 = _rec_inputs()

    def _L0_cond_setup():
        import jax, jax.numpy as jnp
        import numpy as np
        B, T, D, H, TE = (4, 1024, 512, 8, 1024)
        EPS = 1e-05

        def _ln(x, w, b):
            m = jnp.mean(x, axis=-1, keepdims=True)
            v = jnp.mean((x - m) ** 2, axis=-1, keepdims=True)
            return (x - m) * jax.lax.rsqrt(v + EPS) * w + b
        key = jax.random.key(seed)
        ks = jax.random.split(key, 16)
        s = 0.02
        inp = {'x': jax.random.normal(ks[0], (B, T, D), jnp.float32), 'emb': jax.random.normal(ks[1], (B, TE), jnp.float32), 'src_mask': (jax.random.uniform(ks[2], (B, T, 1)) > 0.2).astype(jnp.float32), 'num_head': H, 'ln_w': jnp.ones((D,), jnp.float32), 'ln_b': jnp.zeros((D,), jnp.float32), 'Wq': jax.random.normal(ks[3], (D, D), jnp.float32) * s, 'bq': jnp.zeros((D,), jnp.float32), 'Wk': jax.random.normal(ks[4], (D, D), jnp.float32) * s, 'bk': jnp.zeros((D,), jnp.float32), 'Wv': jax.random.normal(ks[5], (D, D), jnp.float32) * s, 'bv': jnp.zeros((D,), jnp.float32), 'W_emb': jax.random.normal(ks[6], (TE, 2 * D), jnp.float32) * s, 'b_emb': jnp.zeros((2 * D,), jnp.float32), 'ln2_w': jnp.ones((D,), jnp.float32), 'ln2_b': jnp.zeros((D,), jnp.float32), 'W_out': jax.random.normal(ks[7], (D, D), jnp.float32) * s, 'b_out': jnp.zeros((D,), jnp.float32)}
        return inp
    _L0_cond_all = _L0_cond_setup()
    _L0_cond_in = {k: v for k, v in _L0_cond_all.items() if k in ('ln_w', 'ln_b', 'Wq', 'bq', 'Wk', 'bk', 'Wv', 'bv', 'W_emb', 'b_emb', 'ln2_w', 'ln2_b', 'W_out', 'b_out')}
    del _L0_cond_all
    return {'x': x, 'cond_2048': cond_2048, 'mask_BxSx1_fk1': mask_BxSx1_fk1, 'L0_cond_ln_w': _L0_cond_in['ln_w'], 'L0_cond_ln_b': _L0_cond_in['ln_b'], 'L0_cond_Wq': _L0_cond_in['Wq'], 'L0_cond_bq': _L0_cond_in['bq'], 'L0_cond_Wk': _L0_cond_in['Wk'], 'L0_cond_bk': _L0_cond_in['bk'], 'L0_cond_Wv': _L0_cond_in['Wv'], 'L0_cond_bv': _L0_cond_in['bv'], 'L0_cond_W_emb': _L0_cond_in['W_emb'], 'L0_cond_b_emb': _L0_cond_in['b_emb'], 'L0_cond_ln2_w': _L0_cond_in['ln2_w'], 'L0_cond_ln2_b': _L0_cond_in['ln2_b'], 'L0_cond_W_out': _L0_cond_in['W_out'], 'L0_cond_b_out': _L0_cond_in['b_out']}

def reference(x, cond_2048, mask_BxSx1_fk1, L0_cond_ln_w, L0_cond_ln_b, L0_cond_Wq, L0_cond_bq, L0_cond_Wk, L0_cond_bk, L0_cond_Wv, L0_cond_bv, L0_cond_W_emb, L0_cond_b_emb, L0_cond_ln2_w, L0_cond_ln2_b, L0_cond_W_out, L0_cond_b_out):
    import jax
    import jax.numpy as jnp

    def _L0_cond_ref(x, emb, src_mask, num_head, ln_w, ln_b, Wq, bq, Wk, bk, Wv, bv, W_emb, b_emb, ln2_w, ln2_b, W_out, b_out):
        import jax, jax.numpy as jnp
        import numpy as np
        B, T, D, H, TE = (4, 1024, 512, 8, 1024)
        EPS = 1e-05

        def _ln(x, w, b):
            m = jnp.mean(x, axis=-1, keepdims=True)
            v = jnp.mean((x - m) ** 2, axis=-1, keepdims=True)
            return (x - m) * jax.lax.rsqrt(v + EPS) * w + b
        b, t, d = x.shape
        h = num_head
        dh = d // h
        xn = _ln(x, ln_w, ln_b)
        q = xn @ Wq + bq
        k = xn @ Wk + bk + (1.0 - src_mask) * -1000000.0
        q = jax.nn.softmax(q.reshape(b, t, h, dh), axis=-1)
        k = jax.nn.softmax(k.reshape(b, t, h, dh), axis=1)
        v = ((xn @ Wv + bv) * src_mask).reshape(b, t, h, dh)
        att = jnp.einsum('bnhd,bnhl->bhdl', k, v)
        y = jnp.einsum('bnhd,bhdl->bnhl', q, att).reshape(b, t, d)
        emb_out = (jax.nn.silu(emb) @ W_emb + b_emb)[:, None, :]
        scale, shift = jnp.split(emb_out, 2, axis=2)
        hh = _ln(y, ln2_w, ln2_b) * (1.0 + scale) + shift
        hh = jax.nn.silu(hh) @ W_out + b_out
        return x + hh
    x = _L0_cond_ref(x, cond_2048, mask_BxSx1_fk1, 8, L0_cond_ln_w, L0_cond_ln_b, L0_cond_Wq, L0_cond_bq, L0_cond_Wk, L0_cond_bk, L0_cond_Wv, L0_cond_bv, L0_cond_W_emb, L0_cond_b_emb, L0_cond_ln2_w, L0_cond_ln2_b, L0_cond_W_out, L0_cond_b_out)
    return x

_drawn_inputs = setup_inputs


def setup_inputs(seed=0):
    import zlib

    import numpy as np

    out = dict(_drawn_inputs(seed))
    spreads = {'L0_cond_ln_w': (1.0, 0.6),
     'L0_cond_ln_b': (0.0, 0.1),
     'L0_cond_bq': (0.0, 0.8),
     'L0_cond_bk': (0.0, 0.8),
     'L0_cond_bv': (0.0, 0.1),
     'L0_cond_b_emb': (0.0, 0.1),
     'L0_cond_ln2_w': (1.0, 0.2),
     'L0_cond_ln2_b': (0.0, 0.311),
     'L0_cond_b_out': (0.0, 0.1)}
    factors = {'L0_cond_Wq': 8.0, 'L0_cond_Wk': 8.0}
    for name, (base, spread) in spreads.items():
        noise = np.random.default_rng([zlib.crc32(name.encode()), seed]).standard_normal(out[name].shape)
        drawn = base * np.exp(spread * noise) if base else spread * noise
        out[name] = jnp.asarray(drawn.astype(out[name].dtype))
    for name, factor in factors.items():
        out[name] = (out[name] * factor).astype(out[name].dtype)
    return out
```

```python
from contextlib import ExitStack

import concourse.bass as bass
from concourse import mybir

F32 = mybir.dt.float32
F32R = mybir.dt.float32r
U32 = mybir.dt.uint32
I32 = mybir.dt.int32
ALU = mybir.AluOpType
ACT = mybir.ActivationFunctionType
AX_X = mybir.AxisListType.X

P = 128
EPS = 1e-5
MASK_PENALTY = 1e6
RSQRT_SEED = 0x5F3759DF
LEAST = 3.0e38
STAT_STEPS = 21


def cond_linear_attention(nc, x, cond, mask, ln_w, ln_b, wq, bq, wk, bk, wv, bv, w_emb, b_emb,
                          ln2_w, ln2_b, w_out, b_out, out):
    B, S, D = x.shape
    TE = cond.shape[1]
    DH = 64
    NB = D // P
    C = 4 * P
    NT = C // P
    NC = S // C
    NTE = TE // P
    H = D // DH
    YW = P + 2
    assert NT == 4 and NB == 4 and H == 8 and B == 2 and NC >= 4 and NTE == 8

    x_tok = x.rearrange("b (n p) d -> p (b n) d", p=P)
    out_tok = out.rearrange("b (n p) d -> p (b n) d", p=P)
    mask_row = mask.rearrange("b s o -> o (b s)")

    LNW, LNB, BK, LN2W, LN2B, BEMB = 0, NB, 2 * NB, 3 * NB, 4 * NB, 5 * NB
    COND = BEMB + 2 * NB
    ROWS = COND + B * NTE

    with ExitStack() as ctx:
        def sb(name, shape, dt=F32):
            return ctx.enter_context(nc.sbuf_tensor(name, shape, dt))

        def sem(name):
            return ctx.enter_context(nc.semaphore(name))

        ps = ctx.enter_context(nc.psum_tensor("ps", [P, 8, 512], F32))

        wk_hi, wk_lo = sb("wk_hi", [P, NB, D], F32R), sb("wk_lo", [P, NB, D], F32R)
        wq_hi, wq_lo = sb("wq_hi", [P, NB, D], F32R), sb("wq_lo", [P, NB, D], F32R)
        wo_hi, wo_lo = sb("wo_hi", [P, NB, D], F32R), sb("wo_lo", [P, NB, D], F32R)
        wv_sc = sb("wv_sc", [P, NB, D])
        bq_all, bv_all, bo_all = (sb(n, [P, D]) for n in ("bq_all", "bv_all", "bo_all"))
        ident = sb("ident", [P, P])
        ones = sb("ones", [P, P])
        vec_rows = sb("vec_rows", [ROWS, P])
        cols = sb("cols", [P, ROWS])
        semb = sb("semb", [P, NTE, B])
        semb_t = sb("semb_t", [P, B * NTE])
        emb_cols = sb("emb_cols", [P, B, 2 * NB])
        ab_all = sb("ab_all", [P, B, 2, NB])
        ab = sb("ab", [P, 2, NB])

        x_in = sb("x_in", [P, NT, D])
        z = sb("z", [P, NT, D])
        z_hi, z_lo = sb("z_hi", [P, NT, D], F32R), sb("z_lo", [P, NT, D], F32R)
        zT_hi, zT_lo = sb("zT_hi", [P, NB, C], F32R), sb("zT_lo", [P, NB, C], F32R)
        mrow, pen = sb("mrow", [P, C]), sb("pen", [P, C])
        kT = sb("kT", [P, 2, C])
        ekT = sb("ekT", [P, 2, C])
        ekTm = sb("ekTm", [P, NB, C])
        ek_hi, ek_lo = sb("ek_hi", [P, NT, D], F32R), sb("ek_lo", [P, NT, D], F32R)
        qs = sb("qs", [P, 2, D])
        qmax = sb("qmax", [P, 2, H])
        eq = sb("eq", [P, NC * NT, D])
        g_acc = sb("g_acc", [P, NB, D])
        att = sb("att", [P, NB, YW])
        cmax = sb("cmax", [P, NB])
        nmax, nmax_new, dmax, alpha = (sb(n, [P, NB]) for n in ("nmax", "nmax_new", "dmax", "alpha"))
        zs, zs_new = sb("zs", [P, 2, NB]), sb("zs_new", [P, 2, NB])
        rz = sb("rz", [P, NB])

        def stat_tiles(n):
            return {"raw": sb(n + "_raw", [P, NT, 6]), "mv": sb(n + "_mv", [P, NT, 2]),
                    "v": sb(n + "_v", [P, NT]), "bits": sb(n + "_bits", [P, NT], U32),
                    "y": sb(n + "_y", [P, NT], I32), "a": sb(n + "_a", [P, NT]),
                    "b": sb(n + "_b", [P, NT]), "r": sb(n + "_r", [P, NT]),
                    "shift": sb(n + "_shift", [P, NT]), "go": sb(n + "_go", [P, 1])}

        xst, yst = stat_tiles("xst"), stat_tiles("yst")

        res = sb("res", [P, NT, D])
        eq_in = x_in[:]
        eqT = z[:]
        y = ekTm[:]
        hT_hi, hT_lo = ek_hi[:], ek_lo[:]
        u, th = kT[:], ekT[:]
        rec = sb("rec", [P, 2, 2, 2, 2])
        gT = res[:]
        wk_raw, wq_raw, wv_raw, wo_raw = g_acc[:], ekTm[:], wv_sc[:], res[:]
        emb_rows = qs[0:B, :, :].rearrange("b k d -> b (k d)")
        lnb_wide = pen[:].rearrange("p (c d) -> p c d", c=NB)
        wemb_raw = eq[:].rearrange("p n d -> p (n d)").rearrange("p (t e) -> p t e", t=NTE)

        names = """vec_in wk_in wq_in wv_in wo_in wemb_in bias_in ident0 ident_ok ones_ok vec_ps cols_ok
            lnb_ok bk_ps bk_ok bias_ps bias_ok wk_hi_ok wq_hi_ok wv_ok wo_hi_ok wk_lo_ok wq_lo_ok wo_lo_ok
            sig_ok semb_step semb_ok emb_ps emb_ok embT_ps embc_ok ab_step ab_ready cur_ab att0
            x_ok mask_ok pen_ok xstat x_norm z_ok zT_ps zT_hi_ok zT_lo_ok z_hi_ok z_lo_ok
            k_ps k_sum k_cmax k_nmax k_exp k_masked k_shift k_saved k_alpha zs_step
            ek_ps ek_hi_ok ek_lo_ok g_ps g_ok q_ps q_sum q_max q_shift q_exp reset_ok
            rz_ok gT_ps gT_ok att_ps att_step att_ok
            eq_ok eqT_ps eqT_ok y_ps y_rec y_ok ystat y_norm yn_ok ynT_ps u_ok th_ok h_ok h_hi_ok h_lo_ok
            o_ps o_ok res_b""".split()
        s = {n: sem(n) for n in names}
        res_in = [sem(f"res_in{t}") for t in range(NT)]
        stored = [sem(f"stored{t}") for t in range(NT)]

        block = ctx.enter_context(nc.Block())

        @block.sync
        def _(sp):
            def rows(v, at):
                n = v.shape[0] // P
                sp.dma_start(vec_rows[at:at + n, :], v.rearrange("(c p) -> c p", p=P)).then_inc(s["vec_in"], 16)

            def load_x(i):
                sp.dma_start(x_in[:], x_tok[:, bass.ts(i, NT), :]).then_inc(s["x_ok"], 16)

            def load_mask(i):
                sp.dma_start(mrow[:], mask_row[0:1, bass.ts(i, C)].broadcast_to([P, C])).then_inc(s["mask_ok"], 16)

            for v, at in ((ln_w, LNW), (ln_b, LNB), (bk, BK), (ln2_w, LN2W), (ln2_b, LN2B), (b_emb, BEMB)):
                rows(v, at)
            sp.dma_start(vec_rows[COND:ROWS, :], cond.rearrange("b (t p) -> (b t) p", p=P)).then_inc(s["vec_in"], 16)
            for v, to in ((bq, bq_all), (bv, bv_all), (b_out, bo_all)):
                sp.dma_start(to[:], v.rearrange("(o d) -> o d", o=1).broadcast_to([P, D])).then_inc(s["bias_in"], 16)
            for t in range(NTE):
                sp.dma_start(wemb_raw[:, t, :], w_emb[t * P:(t + 1) * P, :]).then_inc(s["wemb_in"], 16)

            def load_eq(c):
                sp.dma_start(eq_in, eq[:, bass.ts(c, NT), :]).then_inc(s["eq_ok"], 16)

            def load_res(g, t):
                sp.dma_start(res[:, t, :], x_tok[:, bass.ds(g * NT + t, 1), :].rearrange("p o d -> p (o d)")).then_inc(res_in[t], 16)

            def next_chunk_loads(i):
                sp.wait_ge(s["z_ok"], NT * i + NT)
                load_x(i + 1)

            def next_mask(i):
                sp.wait_ge(s["k_masked"], NB * i + NB)
                load_mask(i + 1)

            def phase2_chunk(b, c, nxt, nxt2):
                g = b * NC + c
                if nxt2:
                    sp.wait_ge(s["eqT_ps"], NB * g + 2 * NB)
                    load_eq(c + 2)
                for t in range(NT):
                    sp.wait_ge(s["o_ok"], NT * g + t + 1)
                    sp.dma_start(out_tok[:, bass.ds(g * NT + t, 1), :].rearrange("p o d -> p (o d)"),
                                 res[:, t, :]).then_inc(stored[t], 16)
                    if nxt and t:
                        sp.wait_ge(stored[t - 1], 16 * g + 16)
                        load_res(g + 1, t - 1)
                if nxt:
                    sp.wait_ge(stored[NT - 1], 16 * g + 16)
                    load_res(g + 1, NT - 1)

            with sp.Fori(0, B) as b:
                i0 = b * NC
                sp.wait_ge(s["z_ok"], NT * i0)
                sp.wait_ge(s["eqT_ps"], NB * i0)
                load_x(i0)
                sp.wait_ge(s["k_masked"], NB * i0)
                load_mask(i0)
                next_chunk_loads(i0)
                with sp.Fori(0, NC - 2) as c:
                    next_chunk_loads(i0 + c + 1)
                    next_mask(i0 + c)
                next_mask(i0 + NC - 2)
                sp.wait_ge(s["z_ok"], NT * (i0 + NC))
                sp.wait_ge(s["q_exp"], NT * (i0 + NC))
                load_eq(0)
                sp.wait_ge(s["eqT_ps"], NB * i0 + NB)
                load_eq(1)
                sp.wait_ge(s["wo_lo_ok"], NB)
                sp.wait_ge(s["att_ps"], NB * b + NB)
                for t in range(NT):
                    sp.wait_ge(stored[t], 16 * i0)
                    load_res(i0, t)
                with sp.Fori(0, NC - 2) as c:
                    phase2_chunk(b, c, True, True)
                phase2_chunk(b, NC - 2, True, False)
                phase2_chunk(b, NC - 1, False, False)
            for t in range(NT):
                sp.wait_ge(stored[t], 16 * B * NC)

        @block.scalar
        def _(act):
            def copy(o, i, done, scale=1.0):
                act.activation(o, i, ACT.Copy, scale=scale).then_inc(s[done], 1)

            for w, raw, done in ((wk, wk_raw, "wk_in"), (wq, wq_raw, "wq_in"), (wv, wv_raw, "wv_in"), (w_out, wo_raw, "wo_in")):
                act.dma_start(raw, w.rearrange("(c p) n -> p c n", p=P)).then_inc(s[done], 16)

            act.wait_ge(s["cols_ok"], 1)
            act.wait_ge(s["wk_in"], 16)
            for f in range(NB):
                copy(wk_hi[:, f, :], wk_raw[:, f, :], "wk_hi_ok", cols[:, LNW + f:LNW + f + 1])
            act.wait_ge(s["wq_in"], 16)
            for f in range(NB):
                copy(wq_hi[:, f, :], wq_raw[:, f, :], "wq_hi_ok", cols[:, LNW + f:LNW + f + 1])
            act.wait_ge(s["wo_in"], 16)
            for f in range(NB):
                copy(wo_hi[:, f, :], wo_raw[:, f, :], "wo_hi_ok", 0.5)
            act.activation(semb_t[:], cols[:, COND:ROWS], ACT.Tanh, scale=0.5).then_inc(s["sig_ok"], 1)

            act.wait_ge(s["bias_ps"], 2)
            for f in range(NB):
                copy(wv_sc[:, f, :], wv_raw[:, f, :], "wv_ok", cols[:, LNW + f:LNW + f + 1])

            def normalise_x(i):
                act.wait_ge(s["x_norm"], i + 1)
                act.wait_ge(s["z_hi_ok"], NT * i)
                act.wait_ge(s["z_lo_ok"], NT * i)
                act.wait_ge(s["zT_ps"], NB * i)
                for t in range(NT):
                    act.activation(z[:, t, :], x_in[:, t, :], ACT.Identity, bias=xst["shift"][:, t:t + 1],
                                   scale=xst["r"][:, t:t + 1]).then_inc(s["z_ok"], 1)

            def zT_high(i):
                for f in range(NB):
                    act.wait_ge(s["zT_ps"], NB * i + f + 1)
                    copy(zT_hi[:, f, :], ps[:, f, :], "zT_hi_ok")

            def phase1(i, c, nxt):
                for j in range(NB):
                    act.wait_ge(s["z_ok"], NT * i + j + 1)
                    act.wait_ge(s["g_ps"], NB * i)
                    copy(z_hi[:, j, :], z[:, j, :], "z_hi_ok")
                    act.wait_ge(s["k_nmax"], NB * i + j + 1)
                    act.wait_ge(s["k_masked"], NB * i + max(j - 1, 0))
                    act.activation(ekT[:, j % 2, :], kT[:, j % 2, :], ACT.Exp, bias=nmax_new[:, j:j + 1],
                                   accum_out=zs_new[:, 0, j:j + 1]).then_inc(s["k_exp"], 1)
                act.wait_ge(s["k_shift"], i + 1)
                act.activation(alpha[:], dmax[:], ACT.Exp).then_inc(s["k_alpha"], 1)
                if nxt:
                    normalise_x(i + 1)
                for t in range(NT):
                    act.wait_ge(s["q_shift"], NT * i + t + 1)
                    act.activation(eq[:, bass.ds(c * NT + t, 1), :].rearrange("p o d -> p (o d)"), qs[:, t % 2, :],
                                   ACT.Exp).then_inc(s["q_exp"], 1)
                for t in range(NT):
                    act.wait_ge(s["ek_ps"], NT * i + t + 1)
                    copy(ek_hi[:, t, :], ps[:, t, :], "ek_hi_ok")
                if nxt:
                    zT_high(i + 1)

            def turn_q(g):
                for j in range(NB):
                    act.wait_ge(s["eqT_ps"], NB * g + j + 1)
                    copy(eqT[:, j, :], ps[:, j, :], "eqT_ok")

            def normalise_y(g):
                act.wait_ge(s["y_norm"], g + 1)
                for t in range(NT):
                    act.activation(y[:, t, :], y[:, t, :], ACT.Identity, bias=yst["shift"][:, t:t + 1],
                                   scale=yst["r"][:, t:t + 1]).then_inc(s["yn_ok"], 1)

            def silu_high(g):
                def high(f):
                    act.wait_ge(s["h_ok"], NB * g + f + 1)
                    copy(hT_hi[:, f, :], th[:, f % 2, :], "h_hi_ok")

                for f in range(NB):
                    act.wait_ge(s["ynT_ps"], NB * g + f + 1)
                    act.wait_ge(s["h_ok"], NB * g + max(f - 1, 0))
                    act.activation(u[:, f % 2, :], ps[:, f, :], ACT.Identity, bias=ab[:, 1, f:f + 1],
                                   scale=ab[:, 0, f:f + 1]).then_inc(s["u_ok"], 1)
                    act.wait_ge(s["u_ok"], NB * g + f + 1)
                    act.wait_ge(s["h_lo_ok"], NB * g + max(f - 1, 0))
                    act.activation(th[:, f % 2, :], u[:, f % 2, :], ACT.Tanh, scale=0.5).then_inc(s["th_ok"], 1)
                    if f:
                        high(f - 1)
                high(NB - 1)

            with act.Fori(0, B) as b:
                i0 = b * NC
                act.wait_ge(s["y_ps"], NT * i0)
                normalise_x(i0)
                zT_high(i0)
                with act.Fori(0, NC - 1) as c:
                    phase1(i0 + c, c, True)
                phase1(i0 + NC - 1, NC - 1, False)
                act.wait_ge(s["z_lo_ok"], NT * (i0 + NC))
                act.wait_ge(s["z_hi_ok"], NT * (i0 + NC))
                turn_q(i0)
                act.wait_ge(s["wo_lo_ok"], NB)
                for t in range(NT):
                    act.wait_ge(stored[t], 16 * i0)
                for f in range(NB):
                    act.wait_ge(s["gT_ps"], NB * b + f + 1)
                    copy(gT[:, f, :], ps[:, 4 + f, :], "gT_ok")
                turn_q(i0 + 1)
                normalise_y(i0)
                with act.Fori(0, NC - 2) as c:
                    silu_high(i0 + c)
                    turn_q(i0 + c + 2)
                    normalise_y(i0 + c + 1)
                silu_high(i0 + NC - 2)
                normalise_y(i0 + NC - 1)
                silu_high(i0 + NC - 1)

        @block.gpsimd
        def _(pool):
            pool.memset(ident[:], 0.0).then_inc(s["ident0"], 1)
            pool.memset(ones[:], 1.0).then_inc(s["ones_ok"], 1)
            pool.wait_ge(s["ident0"], 1)
            pool.affine_select(out=ident[:], in_=ident[:], compare_op=ALU.not_equal, fill=1.0, base=0,
                               pattern=[[-1, P]], channel_multiplier=1).then_inc(s["ident_ok"], 1)
            pool.wait_ge(s["bias_in"], 48)
            with pool.Fori(0, B * NC) as g:
                for t in range(NT):
                    pool.wait_ge(res_in[t], 16 * g + 16)
                    pool.tensor_tensor(res[:, t, :], res[:, t, :], bo_all[:], ALU.add).then_inc(s["res_b"], 1)

        @block.vector
        def _(dve):
            def rsqrt_stats(src, st, step, base, done):
                n = 0

                def link(ins):
                    nonlocal n
                    n += 1
                    ins.then_inc(s[step], 1)

                def here():
                    dve.wait_ge(s[step], base + n)

                for t in range(NT):
                    link(dve.bn_stats(st["raw"][:, t, :], src[:, t, :]))
                here()
                dve.memset(st["go"][:], 0.0)
                for t in range(NT):
                    link(dve.bn_aggr(st["mv"][:, t, :], st["raw"][:, t, :]))
                here()
                link(dve.tensor_scalar(st["v"][:], st["mv"][:, :, 1], EPS, None, ALU.add))
                here()
                link(dve.tensor_scalar(st["bits"][:], st["v"][:].bitcast(U32), 1, None, ALU.logical_shift_right))
                here()
                link(dve.tensor_scalar(st["y"][:], st["bits"][:], -1.0, float(RSQRT_SEED), ALU.mult, ALU.add))
                root = st["y"][:].bitcast(F32)
                for k in range(3):
                    here()
                    link(dve.scalar_tensor_tensor(out=st["a"][:], in0=root, scalar=-0.5, in1=root, op0=ALU.mult, op1=ALU.mult))
                    here()
                    link(dve.tensor_tensor(st["b"][:], st["a"][:], st["v"][:], ALU.mult))
                    here()
                    link(dve.scalar_tensor_tensor(out=st["r"][:], in0=st["b"][:], scalar=1.5, in1=root, op0=ALU.add, op1=ALU.mult))
                    root = st["r"][:]
                here()
                dve.scalar_tensor_tensor(out=st["shift"][:], in0=st["mv"][:, :, 0], scalar=-1.0, in1=root,
                                         op0=ALU.mult, op1=ALU.mult).then_inc(s[done], 1)
                assert n == STAT_STEPS - 1, n

            dve.memset(att[:], 0.0).then_inc(s["att0"], 1)
            dve.wait_ge(s["att0"], 1)
            dve.memset(att[0:DH, :, P:P + 1], 1.0).then_inc(s["att0"], 1)
            dve.memset(att[DH:P, :, P + 1:P + 2], 1.0).then_inc(s["att0"], 1)
            dve.wait_ge(s["vec_ps"], 1)
            dve.tensor_copy(cols[:], ps[:, 0, 0:ROWS]).then_inc(s["cols_ok"], 1)
            dve.wait_ge(s["cols_ok"], 1)
            dve.wait_ge(s["ones_ok"], 1)
            for f in range(NB):
                dve.tensor_scalar(lnb_wide[:, f, :], ones[:], cols[:, LNB + f:LNB + f + 1], None,
                                  ALU.mult).then_inc(s["lnb_ok"], 1)
            for raw, hi, lo, got, ok in ((wk_raw, wk_hi, wk_lo, "wk_hi_ok", "wk_lo_ok"),
                                         (wq_raw, wq_hi, wq_lo, "wq_hi_ok", "wq_lo_ok")):
                for f in range(NB):
                    dve.wait_ge(s[got], f + 1)
                    dve.scalar_tensor_tensor(out=lo[:, f, :], in0=raw[:, f, :], scalar=cols[:, LNW + f:LNW + f + 1],
                                             in1=hi[:, f, :].bitcast(F32), op0=ALU.mult, op1=ALU.subtract).then_inc(s[ok], 1)
            for f in range(NB):
                dve.wait_ge(s["wo_hi_ok"], f + 1)
                dve.scalar_tensor_tensor(out=wo_lo[:, f, :], in0=wo_raw[:, f, :], scalar=0.5,
                                         in1=wo_hi[:, f, :].bitcast(F32), op0=ALU.mult,
                                         op1=ALU.subtract).then_inc(s["wo_lo_ok"], 1)
            dve.wait_ge(s["bk_ps"], 1)
            dve.tensor_tensor(cols[:, BK:BK + NB], cols[:, BK:BK + NB], ps[:, 3, 0:NB], ALU.add).then_inc(s["bk_ok"], 1)
            dve.wait_ge(s["bias_in"], 48)
            for bank, to in ((1, bq_all), (2, bv_all)):
                dve.wait_ge(s["bias_ps"], bank)
                dve.tensor_tensor(to[:], to[:], ps[:, bank, :], ALU.add).then_inc(s["bias_ok"], 1)
            dve.wait_ge(s["sig_ok"], 1)
            dve.scalar_tensor_tensor(out=semb_t[:], in0=semb_t[:], scalar=1.0, in1=cols[:, COND:ROWS], op0=ALU.add,
                                     op1=ALU.mult).then_inc(s["semb_step"], 1)
            dve.wait_ge(s["semb_step"], 1)
            dve.tensor_scalar(semb[:], semb_t[:].rearrange("p (b t) -> p t b", b=B), 0.5, None,
                              ALU.mult).then_inc(s["semb_ok"], 1)
            dve.wait_ge(s["emb_ps"], 1)
            for h in range(2):
                dve.tensor_copy(emb_rows[:, h * D:(h + 1) * D], ps[0:B, 4 + h, :]).then_inc(s["emb_ok"], 1)
            dve.wait_ge(s["embT_ps"], 1)
            for b in range(B):
                dve.tensor_tensor(emb_cols[:, b, :], ps[:, 6, 0:2 * 2 * NB].rearrange("p (c b) -> p b c", b=B)[:, b, :],
                                  cols[:, BEMB:BEMB + 2 * NB], ALU.add).then_inc(s["embc_ok"], 1)
            dve.wait_ge(s["embc_ok"], B)
            for b in range(B):
                for k, w in ((0, LN2W), (1, LN2B)):
                    dve.scalar_tensor_tensor(out=ab_all[:, b, k, :], in0=emb_cols[:, b, 0:NB], scalar=1.0,
                                             in1=cols[:, w:w + NB], op0=ALU.add, op1=ALU.mult).then_inc(s["ab_step"], 1)
                dve.wait_ge(s["ab_step"], 3 * b + 2)
                dve.tensor_tensor(ab_all[:, b, 1, :], ab_all[:, b, 1, :], emb_cols[:, b, NB:2 * NB],
                                  ALU.add).then_inc(s["ab_step"], 1)
            dve.wait_ge(s["ab_step"], 3 * B)

            def x_stats(i):
                dve.wait_ge(s["x_ok"], 16 * i + 16)
                rsqrt_stats(x_in, xst, "xstat", (STAT_STEPS - 1) * i, "x_norm")

            def penalty(i):
                dve.wait_ge(s["mask_ok"], 16 * i + 16)
                dve.tensor_scalar(pen[:], mrow[:], 1.0, MASK_PENALTY, ALU.subtract, ALU.mult).then_inc(s["pen_ok"], 1)

            def zT_low(i):
                for f in range(NB):
                    dve.wait_ge(s["zT_hi_ok"], NB * i + f + 1)
                    dve.tensor_tensor(zT_lo[:, f, :], ps[:, f, :], zT_hi[:, f, :].bitcast(F32),
                                      ALU.subtract).then_inc(s["zT_lo_ok"], 1)

            def phase1(i, nxt, nxt2, mask_nxt):
                def masked(j):
                    dve.wait_ge(s["k_exp"], NB * i + j + 1)
                    dve.scalar_tensor_tensor(out=ekTm[:, j, :], in0=ekT[:, j % 2, :], scalar=1.0, in1=mrow[:],
                                             op0=ALU.mult, op1=ALU.mult,
                                             accum_out=zs_new[:, 1, j:j + 1]).then_inc(s["k_masked"], 1)

                dve.wait_ge(s["pen_ok"], i + 1)
                for j in range(NB):
                    n = NB * i + j + 1
                    dve.wait_ge(s["k_ps"], n)
                    dve.wait_ge(s["k_exp"], NB * i + max(j - 1, 0))
                    dve.scalar_tensor_tensor(out=kT[:, j % 2, :], in0=ps[:, j, :], scalar=cols[:, BK + j:BK + j + 1],
                                             in1=pen[:], op0=ALU.add, op1=ALU.add).then_inc(s["k_sum"], 1)
                    if j:
                        masked(j - 1)
                    dve.wait_ge(s["k_sum"], n)
                    dve.tensor_reduce(cmax[:, j:j + 1], kT[:, j % 2, :], AX_X, ALU.max, negate=True).then_inc(s["k_cmax"], 1)
                    dve.wait_ge(s["z_hi_ok"], n)
                    dve.tensor_tensor(z_lo[:, j, :], z[:, j, :], z_hi[:, j, :].bitcast(F32),
                                      ALU.subtract).then_inc(s["z_lo_ok"], 1)
                    dve.wait_ge(s["k_cmax"], n)
                    dve.tensor_tensor(nmax_new[:, j:j + 1], nmax[:, j:j + 1], cmax[:, j:j + 1],
                                      ALU.min).then_inc(s["k_nmax"], 1)
                dve.wait_ge(s["k_nmax"], NB * i + NB)
                dve.tensor_tensor(dmax[:], nmax_new[:], nmax[:], ALU.subtract).then_inc(s["k_shift"], 1)
                masked(NB - 1)
                dve.wait_ge(s["k_shift"], i + 1)
                dve.tensor_copy(nmax[:], nmax_new[:]).then_inc(s["k_saved"], 1)
                for t in range(NT):
                    n = NT * i + t + 1
                    dve.wait_ge(s["q_ps"], n)
                    dve.wait_ge(s["q_exp"], NT * i + max(t - 1, 0))
                    dve.tensor_tensor(qs[:, t % 2, :], ps[:, t, :], bq_all[:], ALU.add).then_inc(s["q_sum"], 1)
                    q_heads = qs[:, t % 2, :].rearrange("p (h d) -> p h d", h=H)
                    dve.wait_ge(s["q_sum"], n)
                    dve.tensor_reduce(qmax[:, t % 2, :], q_heads, AX_X, ALU.max).then_inc(s["q_max"], 1)
                    dve.wait_ge(s["q_max"], n)
                    dve.tensor_tensor(q_heads, q_heads, qmax[:, t % 2, :].unsqueeze(2).broadcast_to([P, H, DH]),
                                      ALU.subtract).then_inc(s["q_shift"], 1)
                dve.wait_ge(s["k_alpha"], i + 1)
                dve.wait_ge(s["k_masked"], NB * i + NB)
                dve.tensor_tensor(zs[:], zs[:], alpha[:].unsqueeze(1).broadcast_to([P, 2, NB]), ALU.mult).then_inc(s["zs_step"], 1)
                dve.wait_ge(s["zs_step"], 2 * i + 1)
                dve.tensor_tensor(zs[:], zs[:], zs_new[:], ALU.add).then_inc(s["zs_step"], 1)
                for t in range(NT):
                    dve.wait_ge(s["ek_hi_ok"], NT * i + t + 1)
                    dve.tensor_tensor(ek_lo[:, t, :], ps[:, t, :], ek_hi[:, t, :].bitcast(F32),
                                      ALU.subtract).then_inc(s["ek_lo_ok"], 1)
                if nxt:
                    zT_low(i + 1)
                if nxt2:
                    x_stats(i + 2)
                if nxt:
                    penalty(i + 1)
                for j in range(NB):
                    dve.wait_ge(s["g_ps"], NB * i + j + 1)
                    dve.scalar_tensor_tensor(out=g_acc[:, j, :], in0=g_acc[:, j, :], scalar=alpha[:, j:j + 1],
                                             in1=ps[:, 4 + j, :], op0=ALU.mult, op1=ALU.add).then_inc(s["g_ok"], 1)

            def y_phase(g):
                for t in range(NT):
                    n = NT * g + t + 1
                    bank = 4 + 2 * (t % 2)
                    dve.wait_ge(s["y_ps"], n)
                    dve.wait_ge(s["y_ok"], 2 * (NT * g + max(t - 1, 0)))
                    for k in range(2):
                        half = ps[:, bank + k, 0:2 * YW].rearrange("p (q c) -> p q c", q=2)
                        dve.reciprocal(rec[:, t % 2, k, :, :], half[:, :, P:YW]).then_inc(s["y_rec"], 1)
                    for k in range(2):
                        half = ps[:, bank + k, 0:2 * YW].rearrange("p (q c) -> p q c", q=2)
                        dve.wait_ge(s["y_rec"], 2 * (n - 1) + k + 1)
                        dve.tensor_tensor(y[:, t, k * 2 * P:(k + 1) * 2 * P].rearrange("p (q h d) -> p q h d", q=2, h=2),
                                          half[:, :, 0:P].rearrange("p q (h d) -> p q h d", h=2),
                                          rec[:, t % 2, k, :, :].unsqueeze(3).broadcast_to([P, 2, 2, DH]),
                                          ALU.mult).then_inc(s["y_ok"], 1)
                dve.wait_ge(s["y_ok"], 2 * (NT * g + NT))
                rsqrt_stats(y, yst, "ystat", (STAT_STEPS - 1) * g, "y_norm")

            def silu_low(g):
                def low(f):
                    dve.wait_ge(s["h_hi_ok"], NB * g + f + 1)
                    dve.tensor_tensor(hT_lo[:, f, :], th[:, f % 2, :], hT_hi[:, f, :].bitcast(F32),
                                      ALU.subtract).then_inc(s["h_lo_ok"], 1)

                for f in range(NB):
                    dve.wait_ge(s["th_ok"], NB * g + f + 1)
                    dve.scalar_tensor_tensor(out=th[:, f % 2, :], in0=th[:, f % 2, :], scalar=1.0, in1=u[:, f % 2, :],
                                             op0=ALU.add, op1=ALU.mult).then_inc(s["h_ok"], 1)
                    if f:
                        low(f - 1)
                low(NB - 1)

            def out_phase(g):
                for t in range(NT):
                    dve.wait_ge(s["o_ps"], NT * g + t + 1)
                    dve.wait_ge(s["res_b"], NT * g + t + 1)
                    dve.tensor_tensor(res[:, t, :], ps[:, t, :], res[:, t, :], ALU.add).then_inc(s["o_ok"], 1)

            with dve.Fori(0, B) as b:
                i0 = b * NC
                dve.memset(nmax[:], LEAST)
                dve.memset(zs[:], 0.0)
                dve.memset(g_acc[:], 0.0)
                dve.tensor_copy(ab[:].rearrange("p k c -> p (k c)"), ab_all[:].rearrange("p b k c -> p (b k c)")[
                    :, bass.ts(b, 2 * NB)]).then_inc(s["reset_ok"], 1)
                dve.wait_ge(s["reset_ok"], b + 1)
                x_stats(i0)
                zT_low(i0)
                x_stats(i0 + 1)
                penalty(i0)
                with dve.Fori(0, NC - 2) as c:
                    phase1(i0 + c, True, True, True)
                phase1(i0 + NC - 2, True, False, True)
                phase1(i0 + NC - 1, False, False, False)

                dve.wait_ge(s["zs_step"], 2 * (i0 + NC))
                dve.reciprocal(rz[:], zs[:, 0, :]).then_inc(s["rz_ok"], 1)
                dve.wait_ge(s["rz_ok"], b + 1)
                dve.wait_ge(s["att0"], 3)
                dve.wait_ge(s["att_ps"], NB * b + NB)
                for h in range(2):
                    r = slice(DH * h, DH * h + DH)
                    n = 6 * b + 3 * h
                    bias = qs[r, 0, 0:NB * DH].rearrange("p (q d) -> p q d", q=NB)
                    part = bv_all[r, :].rearrange("p (q h d) -> p q h d", q=NB, h=2)[:, :, h, :]
                    dve.tensor_tensor(bias, part, zs[r, 1, :].unsqueeze(2).broadcast_to([DH, NB, DH]),
                                      ALU.mult).then_inc(s["att_step"], 1)
                    dve.wait_ge(s["att_step"], n + 1)
                    dve.tensor_tensor(bias, bias, ps[r, 0:NB, DH * h:DH * h + DH], ALU.add).then_inc(s["att_step"], 1)
                    dve.wait_ge(s["att_step"], n + 2)
                    dve.tensor_tensor(att[r, :, DH * h:DH * h + DH], bias,
                                      rz[r, :].unsqueeze(2).broadcast_to([DH, NB, DH]), ALU.mult).then_inc(s["att_step"], 1)
                y_phase(i0)
                with dve.Fori(0, NC - 1) as c:
                    silu_low(i0 + c)
                    y_phase(i0 + c + 1)
                    out_phase(i0 + c)
                silu_low(i0 + NC - 1)
                out_phase(i0 + NC - 1)

        @block.tensor
        def _(pe):
            def split_product(o, a, bb, start, stop):
                pe.matmul(o, a[0], bb[0], start=start, stop=False)
                pe.matmul(o, a[0], bb[1], start=False, stop=False)
                return pe.matmul(o, a[1], bb[0], start=False, stop=stop)

            def turn(o, i):
                return pe.transpose(o, i, ident[0:i.shape[0], 0:i.shape[0]])

            def blk(t, n):
                return t[:, n * P:(n + 1) * P]

            pe.wait_ge(s["ident_ok"], 1)
            pe.wait_ge(s["vec_in"], 7 * 16)
            turn(ps[:, 0, 0:ROWS], vec_rows[:]).then_inc(s["vec_ps"], 1)
            pe.wait_ge(s["lnb_ok"], NB)
            pe.wait_ge(s["wk_in"], 16)
            for j in range(NB):
                for f in range(NB):
                    last = pe.matmul(ps[:, 3, j:j + 1], blk(wk_raw[:, f, :], j), lnb_wide[:, f, 0:1],
                                     start=(f == 0), stop=(f == NB - 1))
            last.then_inc(s["bk_ps"], 1)
            for bank, raw, got in ((1, wq_raw, "wq_in"), (2, wv_raw, "wv_in")):
                pe.wait_ge(s[got], 16)
                for f in range(NB):
                    last = pe.matmul(ps[:, bank, :], lnb_wide[:, f, :], raw[:, f, :], start=(f == 0), stop=(f == NB - 1))
                last.then_inc(s["bias_ps"], 1)
            pe.wait_ge(s["semb_ok"], 1)
            pe.wait_ge(s["wemb_in"], 16 * NTE)
            for h in range(2):
                for t in range(NTE):
                    last = pe.matmul(ps[0:B, 4 + h, :], semb[:, t, :], wemb_raw[:, t, h * D:(h + 1) * D],
                                     start=(t == 0), stop=(t == NTE - 1))
            last.then_inc(s["emb_ps"], 1)
            pe.wait_ge(s["emb_ok"], 2)
            for k in range(2 * NB):
                last = turn(ps[:, 6, B * k:B * k + B], blk(emb_rows, k))
            last.then_inc(s["embT_ps"], 1)

            def turn_z(i):
                pe.wait_ge(s["z_ok"], NT * i + NT)
                for f in range(NB):
                    for t in range(NT):
                        last = turn(blk(ps[:, f, :], t), blk(z[:, t, :], f))
                    last.then_inc(s["zT_ps"], 1)

            def phase1(i, nxt):
                for j in range(NB):
                    for f in range(NB):
                        if j == 0:
                            pe.wait_ge(s["zT_lo_ok"], NB * i + f + 1)
                        last = split_product(ps[:, j, :], (blk(wk_hi[:, f, :], j), blk(wk_lo[:, f, :], j)),
                                             (zT_hi[:, f, :], zT_lo[:, f, :]), f == 0, f == NB - 1)
                    last.then_inc(s["k_ps"], 1)
                for t in range(NT):
                    pe.wait_ge(s["k_sum"], NB * i + t + 1)
                    for f in range(NB):
                        last = split_product(ps[:, t, :], (blk(zT_hi[:, f, :], t), blk(zT_lo[:, f, :], t)),
                                             (wq_hi[:, f, :], wq_lo[:, f, :]), f == 0, f == NB - 1)
                    last.then_inc(s["q_ps"], 1)
                pe.wait_ge(s["k_masked"], NB * i + NB)
                for t in range(NT):
                    pe.wait_ge(s["q_sum"], NT * i + t + 1)
                    for j in range(NB):
                        last = turn(blk(ps[:, t, :], j), blk(ekTm[:, j, :], t))
                    last.then_inc(s["ek_ps"], 1)
                if nxt:
                    pe.wait_ge(s["z_ok"], NT * i + 2 * NT)
                    for f in range(NB):
                        pe.wait_ge(s["ek_lo_ok"], NT * i + f + 1)
                        for t in range(NT):
                            last = turn(blk(ps[:, f, :], t), blk(z[:, t, :], f))
                        last.then_inc(s["zT_ps"], 1)
                pe.wait_ge(s["g_ok"], NB * i)
                for t in range(NT):
                    pe.wait_ge(s["z_lo_ok"], NT * i + t + 1)
                    pe.wait_ge(s["ek_lo_ok"], NT * i + t + 1)
                    for j in range(NB):
                        last = split_product(ps[:, 4 + j, :], (blk(ek_hi[:, t, :], j), blk(ek_lo[:, t, :], j)),
                                             (z_hi[:, t, :], z_lo[:, t, :]), t == 0, t == NT - 1)
                        if t == NT - 1:
                            last.then_inc(s["g_ps"], 1)

            def turn_q(g, free):
                pe.wait_ge(s["eq_ok"], 16 * g + 16)
                for j in range(NB):
                    free(j)
                    for t in range(NT):
                        last = turn(blk(ps[:, j, :], t), blk(eq_in[:, t, :], j))
                    last.then_inc(s["eqT_ps"], 1)

            def products_y(g):
                pe.wait_ge(s["eqT_ok"], NB * g + NB)
                for t in range(NT):
                    pe.wait_ge(s["y_ok"], 2 * (NT * g + max(t - 1, 0)))
                    for q in range(NB):
                        bank, at = 4 + 2 * (t % 2) + q // 2, (q % 2) * YW
                        last = pe.matmul(ps[:, bank, at:at + YW], blk(eqT[:, q, :], t), att[:, q, :], start=True, stop=True)
                    last.then_inc(s["y_ps"], 1)

            def turn_y(g):
                pe.wait_ge(s["yn_ok"], NT * g + NT)
                pe.wait_ge(s["o_ok"], NT * g)
                for f in range(NB):
                    for t in range(NT):
                        last = turn(blk(ps[:, f, :], t), blk(y[:, t, :], f))
                    last.then_inc(s["ynT_ps"], 1)

            def products_out(g, free):
                for t in range(NT):
                    free(t)
                    for f in range(NB):
                        if t == 0:
                            pe.wait_ge(s["h_lo_ok"], NB * g + f + 1)
                        last = split_product(ps[:, t, :], (blk(hT_hi[:, f, :], t), blk(hT_lo[:, f, :], t)),
                                             (wo_hi[:, f, :], wo_lo[:, f, :]), f == 0, f == NB - 1)
                    last.then_inc(s["o_ps"], 1)

            pe.wait_ge(s["ab_step"], 3 * B)
            pe.wait_ge(s["bk_ok"], 1)
            pe.wait_ge(s["bias_ok"], 2)
            pe.wait_ge(s["wk_lo_ok"], NB)
            pe.wait_ge(s["wq_lo_ok"], NB)
            with pe.Fori(0, B) as b:
                i0 = b * NC
                pe.wait_ge(s["o_ok"], NT * i0)
                turn_z(i0)
                with pe.Fori(0, NC - 1) as c:
                    phase1(i0 + c, True)
                phase1(i0 + NC - 1, False)

                pe.wait_ge(s["ek_lo_ok"], NT * (i0 + NC))
                turn_q(i0, lambda j: None)
                pe.wait_ge(s["g_ok"], NB * (i0 + NC))
                for f in range(NB):
                    for j in range(NB):
                        last = turn(blk(ps[:, 4 + f, :], j), blk(g_acc[:, j, :], f))
                    last.then_inc(s["gT_ps"], 1)
                pe.wait_ge(s["eqT_ok"], NB * i0 + NB)
                pe.wait_ge(s["gT_ok"], NB * b + NB)
                pe.wait_ge(s["wv_ok"], NB)
                for q in range(NB):
                    for f in range(NB):
                        last = pe.matmul(ps[:, q, 0:P], blk(gT[:, f, :], q), blk(wv_sc[:, f, :], q),
                                         start=(f == 0), stop=(f == NB - 1))
                    last.then_inc(s["att_ps"], 1)
                pe.wait_ge(s["att_step"], 6 * b + 6)
                products_y(i0)
                turn_q(i0 + 1, lambda j: None)
                with pe.Fori(0, NC - 2) as c:
                    g = i0 + c
                    pe.wait_ge(s["eqT_ok"], NB * g + 2 * NB)
                    turn_y(g)
                    products_y(g + 1)
                    turn_q(g + 2, lambda j: pe.wait_ge(s["u_ok"], NB * g + j + 1))
                    products_out(g, lambda t: pe.wait_ge(s["eqT_ok"], NB * g + 2 * NB + t + 1))
                g = i0 + NC - 2
                pe.wait_ge(s["eqT_ok"], NB * g + 2 * NB)
                turn_y(g)
                products_y(g + 1)
                products_out(g, lambda t: pe.wait_ge(s["u_ok"], NB * g + t + 1))
                turn_y(g + 1)
                products_out(g + 1, lambda t: pe.wait_ge(s["u_ok"], NB * g + NB + t + 1))


_INS = ["x", "cond_2048", "mask_BxSx1_fk1"] + ["L0_cond_" + n for n in (
    "ln_w", "ln_b", "Wq", "bq", "Wk", "bk", "Wv", "bv", "W_emb", "b_emb", "ln2_w", "ln2_b", "W_out", "b_out")]


def kernel(**inputs):
    import numpy as _np
    import concourse.bacc as _bacc
    from concourse import mybir as _mybir
    from concourse.bass_utils import run_bass_kernel_spmd as _run

    nc = _bacc.Bacc("TRN2", target_bir_lowering=False, num_devices=1)
    arrays, args = {}, []
    for name in _INS:
        a = _np.ascontiguousarray(inputs[name])
        arrays[f"in_{name}_dram"] = a
        args.append(nc.dram_tensor(f"in_{name}_dram", a.shape, _mybir.dt.from_np(a.dtype), kind="ExternalInput").ap())
    shape = _np.shape(inputs["x"])
    args.append(nc.dram_tensor("out_dram", shape, _mybir.dt.float32, kind="ExternalOutput").ap())
    cond_linear_attention(nc, *args)
    r = _run(nc, [arrays], core_ids=[0])
    return r.results[0]["out_dram"]
```

```python
from contextlib import ExitStack

import concourse.bass as bass
from concourse import mybir

F32 = mybir.dt.float32
F32R = mybir.dt.float32r
U32 = mybir.dt.uint32
I32 = mybir.dt.int32
ALU = mybir.AluOpType
ACT = mybir.ActivationFunctionType
AX_X = mybir.AxisListType.X

P = 128
EPS = 1e-5
MASK_PENALTY = 1e6
RSQRT_SEED = 0x5F3759DF
LEAST = 3.0e38
STAT_STEPS = 20


def cond_linear_attention(nc, x, cond, mask, ln_w, ln_b, wq, bq, wk, bk, wv, bv, w_emb, b_emb,
                          ln2_w, ln2_b, w_out, b_out, out):
    B, S, D = x.shape
    TE = cond.shape[1]
    DH = 64
    NB = D // P
    C = 4 * P
    NT = C // P
    NC = S // C
    NTE = TE // P
    H = D // DH
    YW = P + 2
    YS = 2 * P
    assert NT == 4 and NB == 4 and H == 8 and B == 2 and NC == 4 and NTE == 8

    x_tok = x.rearrange("b (n p) d -> p (b n) d", p=P)
    out_tok = out.rearrange("b (n p) d -> p (b n) d", p=P)
    mask_row = mask.rearrange("b s o -> o (b s)")

    LNW, LNB, BK, LN2W, LN2B, BEMB = 0, NB, 2 * NB, 3 * NB, 4 * NB, 5 * NB
    COND = BEMB + 2 * NB
    ROWS = COND + B * NTE
    FIRST = BK

    with ExitStack() as ctx:
        def sb(name, shape, dt=F32):
            return ctx.enter_context(nc.sbuf_tensor(name, shape, dt))

        def sem(name):
            return ctx.enter_context(nc.semaphore(name))

        ps = ctx.enter_context(nc.psum_tensor("ps", [P, 8, 512], F32))
        A, BB = 0, 4

        wk_hi, wk_lo = sb("wk_hi", [P, NB, D], F32R), sb("wk_lo", [P, NB, D], F32R)
        wq_hi, wq_lo = sb("wq_hi", [P, NB, D], F32R), sb("wq_lo", [P, NB, D], F32R)
        wo_hi, wo_lo = sb("wo_hi", [P, NB, D], F32R), sb("wo_lo", [P, NB, D], F32R)
        wv_sc = sb("wv_sc", [P, NB, D])
        bq_all, bv_all, bo_all = (sb(n, [P, D]) for n in ("bq_all", "bv_all", "bo_all"))
        ident = sb("ident", [P, P])
        ln_rows = sb("ln_rows", [FIRST, P])
        vec_rows = sb("vec_rows", [ROWS - FIRST, P])
        cols = sb("cols", [P, ROWS])
        semb = sb("semb", [P, NTE, B])
        semb_t = sb("semb_t", [P, B * NTE])
        emb_cols = sb("emb_cols", [P, B, 2 * NB])
        ab = sb("ab", [P, B, 2, NB])

        x_in = sb("x_in", [P, NT, D])
        z = sb("z", [P, NT, D])
        z_hi, z_lo = sb("z_hi", [P, NT, D], F32R), sb("z_lo", [P, NT, D], F32R)
        zT_hi, zT_lo = sb("zT_hi", [P, NB, C], F32R), sb("zT_lo", [P, NB, C], F32R)
        mrow, pen = sb("mrow", [P, C]), sb("pen", [P, C])
        pen_bias = sb("pen_bias", [P, 2, C])
        kT = sb("kT", [P, 2, C])
        ekT = sb("ekT", [P, 2, C])
        ekTm = sb("ekTm", [P, NB, C])
        ek_hi, ek_lo = sb("ek_hi", [P, NT, D], F32R), sb("ek_lo", [P, NT, D], F32R)
        qs = sb("qs", [P, 2, D])
        qmax = sb("qmax", [P, 2, H])
        eq = sb("eq", [P, NC * NT, D])
        g_acc = sb("g_acc", [P, NB, D])
        att = sb("att", [P, NB, YW])
        kmax, kmax_new, nmax, dmax, alpha = (sb(n, [P, NB]) for n in ("kmax", "kmax_new", "nmax", "dmax", "alpha"))
        zs, zs_new = sb("zs", [P, 2, NB]), sb("zs_new", [P, 2, NB])
        rz = sb("rz", [P, NB])

        def stat_tiles(n):
            return {"raw": sb(n + "_raw", [P, NT, 6]), "mv": sb(n + "_mv", [P, NT, 2]),
                    "v": sb(n + "_v", [P, NT]), "bits": sb(n + "_bits", [P, NT], U32),
                    "y": sb(n + "_y", [P, NT], I32), "a": sb(n + "_a", [P, NT]),
                    "b": sb(n + "_b", [P, NT]), "r": sb(n + "_r", [P, NT]),
                    "shift": sb(n + "_shift", [P, NT])}

        xst, yst = stat_tiles("xst"), [stat_tiles("yst0"), stat_tiles("yst1")]
        go = sb("go", [P, 1])

        res = sb("res", [P, NT, D])
        rec = sb("rec", [P, 2, H])
        gT = res[:]

        def eqT(g):
            return g_acc[:] if g == NC + 1 else z[:]

        y = [ekTm[:], x_in[:], ekTm[:], ekTm[:]]
        hT = [(ek_hi[:], ek_lo[:]), (z_hi[:], z_lo[:])]
        u = [kT[:, 0, :], kT[:, 1, :], qs[:, 0, :], qs[:, 1, :]]
        th = [ekT[:, 0, :], ekT[:, 1, :], pen_bias[:, 0, :], pen_bias[:, 1, :]]
        wemb = [kT[:, 0, :], kT[:, 1, :], ekT[:, 0, :], ekT[:, 1, :], pen_bias[:, 0, :], pen_bias[:, 1, :]] + \
            [x_in[:, t, :] for t in range(NT)]
        NW = len(wemb)
        emb_rows = g_acc[0:B, 0:2, :].rearrange("b k d -> b (k d)")
        wk_raw, wq_raw, wv_raw, wo_raw = g_acc[:], ekTm[:], wv_sc[:], res[:]
        bk_rows = qs[:, 0, :]
        ones = eq[:, 0, 0:P]
        lnb_wide = qs[:, 1, :].rearrange("p (c d) -> p c d", c=NB)

        names = """ln_in vec_in wk_in wq_in wv_in wo_in bias_in ident0 ident_ok ones_ok vec_ps cols_ok
            lnb_ok bias_ps bk_row_ok bk_ps bk_ok bq_ok wk_hi_ok wq_hi_ok wv_ok wo_hi_ok wk_lo_ok wq_lo_ok wo_lo_ok
            sig_ok semb_step semb_ok emb_ps emb_ok embT_ps embc_ok ab_step att0
            x_ok mask_ok pen_ok penb_ok xstat x_norm z_ok zT_ps zT_hi_ok zT_lo_ok z_hi_ok z_lo_ok
            k_ps k_max k_nmax k_exp k_masked k_shift k_saved k_alpha zs_step
            ek_ps ek_hi_ok ek_lo_ok g_ps g_ok q_ps q_sum q_max q_shift q_exp reset_ok
            rz_ok gT_ps gT_ok att_ps att_step
            eqT_ps eqT_ok y_ps y_rec y_ok ystat y_norm yn_ok ynT_ps u_ok th_ok h_ok h_hi_ok h_lo_ok
            o_ps o_ok res_b""".split()
        s = {n: sem(n) for n in names}
        res_in = [sem(f"res_in{t}") for t in range(NT)]
        stored = [sem(f"stored{t}") for t in range(NT)]
        wemb_in = [sem(f"wemb_in{n}") for n in range(2 * NTE)]

        def blk(t, n):
            return t[:, n * P:(n + 1) * P]

        block = ctx.enter_context(nc.Block())

        @block.sync
        def _(sp):
            def load_x(i):
                sp.dma_start(x_in[:], x_tok[:, bass.ts(i, NT), :]).then_inc(s["x_ok"], 16)

            def load_mask(i):
                sp.dma_start(mrow[:], mask_row[0:1, bass.ts(i, C)].broadcast_to([P, C])).then_inc(s["mask_ok"], 16)

            def load_res(g, t):
                sp.dma_start(res[:, t, :], x_tok[:, NT * g + t, :]).then_inc(res_in[t], 16)

            def load_wemb(first, end):
                for n in range(first, end):
                    h, t = n // NTE, n % NTE
                    sp.dma_start(wemb[n % NW], w_emb[t * P:(t + 1) * P, h * D:(h + 1) * D]).then_inc(wemb_in[n], 16)

            def next_x(i):
                sp.wait_ge(s["z_ok"], NT * i + NT)
                load_x(i + 1)

            def next_mask(i):
                sp.wait_ge(s["k_masked"], NB * i + NB)
                load_mask(i + 1)

            for v, at in ((ln_w, LNW), (ln_b, LNB)):
                sp.dma_start(ln_rows[at:at + NB, :], v.rearrange("(c p) -> c p", p=P)).then_inc(s["ln_in"], 16)
            for v, at in ((bk, BK), (ln2_w, LN2W), (ln2_b, LN2B), (b_emb, BEMB)):
                n = v.shape[0] // P
                sp.dma_start(vec_rows[at - FIRST:at - FIRST + n, :], v.rearrange("(c p) -> c p", p=P)).then_inc(s["vec_in"], 16)
            sp.dma_start(vec_rows[COND - FIRST:, :], cond.rearrange("b (t p) -> (b t) p", p=P)).then_inc(s["vec_in"], 16)
            load_mask(0)
            for v, to in ((bq, bq_all), (bv, bv_all), (b_out, bo_all)):
                sp.dma_start(to[:], v.rearrange("(o d) -> o d", o=1).broadcast_to([P, D])).then_inc(s["bias_in"], 16)
            sp.dma_start(wo_raw, w_out.rearrange("(c p) n -> p c n", p=P)).then_inc(s["wo_in"], 16)
            for b in range(B):
                i0 = b * NC
                if b == 0:
                    next_x(0)
                next_mask(i0)
                with sp.Fori(1, NC - 1) as c:
                    next_x(i0 + c)
                    next_mask(i0 + c)
                if b == 0:
                    sp.wait_ge(s["k_masked"], NB * NC)
                    sp.wait_ge(s["z_ok"], NT * NC)
                    load_mask(NC)
                    load_wemb(0, NW)
                    sp.wait_ge(s["emb_ps"], 1)
                    load_wemb(NW, 2 * NTE)
                sp.wait_ge(s["att_ps"], b + 1)
                for t in range(NT):
                    load_res(i0, t)
                for g in range(i0, i0 + NC):
                    for t in range(NT):
                        sp.wait_ge(s["o_ok"], NT * g + t + 1)
                        sp.dma_start(out_tok[:, NT * g + t, :], res[:, t, :]).then_inc(stored[t], 16)
                        if g + 1 < i0 + NC:
                            if t:
                                sp.wait_ge(stored[t - 1], 16 * g + 16)
                                load_res(g + 1, t - 1)
                    if g + 1 < i0 + NC:
                        sp.wait_ge(stored[NT - 1], 16 * g + 16)
                        load_res(g + 1, NT - 1)
                    if g == i0 and b + 1 < B:
                        sp.wait_ge(s["ynT_ps"], NB * (g + 2))
                        load_x(i0 + NC)
                    if g == i0 + 2 and b + 1 < B:
                        next_x(i0 + NC)
            for t in range(NT):
                sp.wait_ge(stored[t], 16 * B * NC)

        @block.scalar
        def _(act):
            def copy(o, i, done, scale=1.0):
                act.activation(o, i, ACT.Copy, scale=scale).then_inc(s[done], 1)

            def ln_weight(f):
                return cols[:, LNW + f:LNW + f + 1]

            act.dma_start(x_in[:], x_tok[:, 0:NT, :]).then_inc(s["x_ok"], 16)
            for w, raw, done in ((wk, wk_raw, "wk_in"), (wq, wq_raw, "wq_in"), (wv, wv_raw, "wv_in")):
                act.dma_start(raw, w.rearrange("(c p) n -> p c n", p=P)).then_inc(s[done], 16)

            def normalise_x(i, z_read=False):
                act.wait_ge(s["x_norm"], i + 1)
                if z_read:
                    act.wait_ge(s["z_hi_ok"], NT * i)
                for t in range(NT):
                    if z_read:
                        act.wait_ge(s["z_lo_ok"], NT * (i - 1) + t + 1)
                    act.activation(z[:, t, :], x_in[:, t, :], ACT.Identity, bias=xst["shift"][:, t:t + 1],
                                   scale=xst["r"][:, t:t + 1]).then_inc(s["z_ok"], 1)

            def zT_high(i, bank):
                for f in range(NB):
                    act.wait_ge(s["zT_ps"], NB * i + f + 1)
                    copy(zT_hi[:, f, :], ps[:, bank + f, :], "zT_hi_ok")

            def z_high(i):
                for t in range(NT):
                    act.wait_ge(s["z_ok"], NT * i + t + 1)
                    copy(z_hi[:, t, :], z[:, t, :], "z_hi_ok")

            def k_phase(i):
                def pen_with_bias(j):
                    if j < 2:
                        act.wait_ge(s["pen_ok"], i + 1)
                    else:
                        act.wait_ge(s["k_max"], NB * i + j - 1)
                    act.activation(pen_bias[:, j % 2, :], pen[:], ACT.Identity,
                                   bias=cols[:, BK + j:BK + j + 1]).then_inc(s["penb_ok"], 1)

                def exp_k(j):
                    act.wait_ge(s["k_nmax"], NB * i + j + 1)
                    if j >= 2:
                        act.wait_ge(s["k_masked"], NB * i + j - 1)
                    act.activation(ekT[:, j % 2, :], kT[:, j % 2, :], ACT.Exp, bias=nmax[:, j:j + 1],
                                   accum_out=zs_new[:, 0, j:j + 1]).then_inc(s["k_exp"], 1)

                pen_with_bias(0)
                pen_with_bias(1)
                exp_k(0)
                pen_with_bias(2)
                exp_k(1)
                pen_with_bias(3)
                exp_k(2)
                exp_k(3)

            def exp_q(i, c, t):
                act.wait_ge(s["q_shift"], NT * i + t + 1)
                to = eq[:, c * NT + t, :] if isinstance(c, int) else \
                    eq[:, bass.ds(c * NT + t, 1), :].rearrange("p o d -> p (o d)")
                act.activation(to, qs[:, t % 2, :], ACT.Exp).then_inc(s["q_exp"], 1)

            def ek_high(i):
                for t in range(NT):
                    act.wait_ge(s["ek_ps"], NT * i + t + 1)
                    copy(ek_hi[:, t, :], ps[:, A + t, :], "ek_hi_ok")

            def phase1(i, c, first, last):
                if first:
                    z_high(i)
                    k_phase(i)
                    normalise_x(i + 1, z_read=True)
                else:
                    k_phase(i)
                    act.wait_ge(s["g_ps"], NB * i)
                    z_high(i)
                act.wait_ge(s["k_shift"], i + 1)
                act.activation(alpha[:], dmax[:], ACT.Exp).then_inc(s["k_alpha"], 1)
                exp_q(i, c, 0)
                if last:
                    ek_high(i)
                    exp_q(i, c, 1)
                else:
                    if not first:
                        normalise_x(i + 1, z_read=True)
                    exp_q(i, c, 1)
                    exp_q(i, c, 2)
                    zT_high(i + 1, BB)
                    exp_q(i, c, 3)
                    ek_high(i)

            def turn_q(g):
                for j in range(NB):
                    act.wait_ge(s["eqT_ps"], NB * g + j + 1)
                    copy(eqT(g)[:, j, :], ps[:, BB + j, :], "eqT_ok")

            def normalise_y(g):
                act.wait_ge(s["y_norm"], g + 1)
                for t in range(NT):
                    y_t = y[g % NC][:, t, :]
                    act.activation(y_t, y_t, ACT.Identity, bias=yst[g % 2]["shift"][:, t:t + 1],
                                   scale=yst[g % 2]["r"][:, t:t + 1]).then_inc(s["yn_ok"], 1)

            def scale_shift(b, g):
                act.wait_ge(s["ab_step"], 3 * B)
                for f in range(NB):
                    act.wait_ge(s["ynT_ps"], NB * g + f + 1)
                    act.activation(u[f], ps[:, BB + f, :], ACT.Identity, bias=ab[:, b, 1, f:f + 1],
                                   scale=ab[:, b, 0, f:f + 1]).then_inc(s["u_ok"], 1)
                for f in range(NB):
                    act.wait_ge(s["u_ok"], NB * g + f + 1)
                    if g:
                        act.wait_ge(s["h_lo_ok"], NB * (g - 1) + f + 1)
                    act.activation(th[f], u[f], ACT.Tanh, scale=0.5).then_inc(s["th_ok"], 1)

            def h_high(g):
                for f in range(NB):
                    act.wait_ge(s["h_ok"], NB * g + f + 1)
                    copy(hT[g % 2][0][:, f, :], th[f], "h_hi_ok")

            act.wait_ge(s["cols_ok"], 1)
            act.wait_ge(s["wk_in"], 16)
            for f in range(NB):
                copy(wk_hi[:, f, :], wk_raw[:, f, :], "wk_hi_ok", ln_weight(f))
            normalise_x(0)
            zT_high(0, BB)
            act.wait_ge(s["wq_in"], 16)
            for f in range(NB):
                copy(wq_hi[:, f, :], wq_raw[:, f, :], "wq_hi_ok", ln_weight(f))
            act.wait_ge(s["bk_ok"], 1)

            for b in range(B):
                i0 = b * NC
                phase1(i0, 0, True, False)
                if b == 0:
                    act.activation(semb_t[:], cols[:, COND:ROWS], ACT.Tanh, scale=0.5).then_inc(s["sig_ok"], 1)
                    act.wait_ge(s["wo_in"], 16)
                    for f in range(NB):
                        copy(wo_hi[:, f, :], wo_raw[:, f, :], "wo_hi_ok", 0.5)
                    act.wait_ge(s["bias_ps"], 3)
                    for f in range(NB):
                        copy(wv_sc[:, f, :], wv_raw[:, f, :], "wv_ok", ln_weight(f))
                with act.Fori(1, NC - 1) as c:
                    phase1(i0 + c, c, False, False)
                phase1(i0 + NC - 1, NC - 1, False, True)

                act.wait_ge(s["z_hi_ok"], NT * (i0 + NC))
                act.wait_ge(s["z_lo_ok"], NT * (i0 + NC))
                turn_q(i0)
                act.wait_ge(s["wo_lo_ok"], NB)
                if b:
                    for t in range(NT):
                        act.wait_ge(stored[t], 16 * i0)
                for f in range(NB):
                    act.wait_ge(s["gT_ps"], NB * b + f + 1)
                    copy(gT[:, f, :], ps[:, BB + f, :], "gT_ok")
                exp_q(i0 + NC - 1, NC - 1, 2)
                exp_q(i0 + NC - 1, NC - 1, 3)
                if b == 0:
                    act.wait_ge(s["y_ps"], NT * (i0 + 1))
                turn_q(i0 + 1)
                normalise_y(i0)
                act.wait_ge(s["y_ps"], NT * (i0 + 2))
                turn_q(i0 + 2)
                scale_shift(b, i0)
                normalise_y(i0 + 1)
                act.wait_ge(s["y_ps"], NT * (i0 + 3))
                turn_q(i0 + 3)
                h_high(i0)
                for g in range(i0 + 1, i0 + NC):
                    scale_shift(b, g)
                    if g + 1 < i0 + NC:
                        normalise_y(g + 1)
                    elif b + 1 < B:
                        act.wait_ge(s["y_ps"], NT * (i0 + NC))
                        normalise_x(i0 + NC)
                    h_high(g)
                if b + 1 < B:
                    zT_high(i0 + NC, A)
                    act.wait_ge(s["o_ps"], NT * (i0 + NC))

        @block.gpsimd
        def _(pool):
            pool.memset(ident[:], 0.0).then_inc(s["ident0"], 1)
            pool.wait_ge(s["ident0"], 1)
            pool.affine_select(out=ident[:], in_=ident[:], compare_op=ALU.not_equal, fill=1.0, base=0,
                               pattern=[[-1, P]], channel_multiplier=1).then_inc(s["ident_ok"], 1)
            pool.wait_ge(s["bias_in"], 48)
            for b in range(B):
                with pool.Fori(b * NC, b * NC + NC) as i:
                    for t in range(NT):
                        pool.wait_ge(s["z_hi_ok"], NT * i + t + 1)
                        pool.tensor_tensor(z_lo[:, t, :], z[:, t, :], z_hi[:, t, :].bitcast(F32),
                                           ALU.subtract).then_inc(s["z_lo_ok"], 1)
                with pool.Fori(b * (NC // 2), b * (NC // 2) + NC // 2) as pair:
                    for k in range(2):
                        g = 2 * pair + k
                        for f in range(NB):
                            pool.wait_ge(s["h_hi_ok"], NB * g + f + 1)
                            pool.tensor_tensor(hT[k][1][:, f, :], th[f], hT[k][0][:, f, :].bitcast(F32),
                                               ALU.subtract).then_inc(s["h_lo_ok"], 1)
                        for t in range(NT):
                            pool.wait_ge(res_in[t], 16 * g + 16)
                            pool.tensor_tensor(res[:, t, :], res[:, t, :], bo_all[:], ALU.add).then_inc(s["res_b"], 1)

        @block.vector
        def _(dve):
            def carry():
                dve.memset(go[:], 0.0)

            def tile_stats(src, st, t, step):
                dve.bn_stats(st["raw"][:, t, :], src[:, t, :]).then_inc(s[step], 1)

            def finish_stats(st, step, base, done, between=lambda k: None):
                n = NT

                def link(ins):
                    nonlocal n
                    n += 1
                    ins.then_inc(s[step], 1)

                def here():
                    between(n - 2 * NT)
                    dve.wait_ge(s[step], base + n)

                dve.wait_ge(s[step], base + NT)
                carry()
                for t in range(NT):
                    link(dve.bn_aggr(st["mv"][:, t, :], st["raw"][:, t, :]))
                here()
                link(dve.tensor_scalar(st["v"][:], st["mv"][:, :, 1], EPS, None, ALU.add))
                here()
                link(dve.tensor_scalar(st["bits"][:], st["v"][:].bitcast(U32), 1, None, ALU.logical_shift_right))
                here()
                link(dve.tensor_scalar(st["y"][:], st["bits"][:], -1.0, float(RSQRT_SEED), ALU.mult, ALU.add))
                root = st["y"][:].bitcast(F32)
                for k in range(3):
                    here()
                    link(dve.scalar_tensor_tensor(out=st["a"][:], in0=root, scalar=-0.5, in1=root, op0=ALU.mult, op1=ALU.mult))
                    here()
                    link(dve.tensor_tensor(st["b"][:], st["a"][:], st["v"][:], ALU.mult))
                    here()
                    link(dve.scalar_tensor_tensor(out=st["r"][:], in0=st["b"][:], scalar=1.5, in1=root, op0=ALU.add, op1=ALU.mult))
                    root = st["r"][:]
                here()
                dve.scalar_tensor_tensor(out=st["shift"][:], in0=st["mv"][:, :, 0], scalar=-1.0, in1=root,
                                         op0=ALU.mult, op1=ALU.mult).then_inc(s[done], 1)
                assert n == STAT_STEPS, n

            def x_stats(i):
                dve.wait_ge(s["x_ok"], 16 * i + 16)
                for t in range(NT):
                    tile_stats(x_in, xst, t, "xstat")
                finish_stats(xst, "xstat", STAT_STEPS * i, "x_norm")

            def penalty(i):
                dve.wait_ge(s["mask_ok"], 16 * i + 16)
                if not isinstance(i, int) or i:
                    dve.wait_ge(s["penb_ok"], NB * i)
                dve.tensor_scalar(pen[:], mrow[:], 1.0, MASK_PENALTY, ALU.subtract, ALU.mult).then_inc(s["pen_ok"], 1)

            def zT_low(i, bank):
                for f in range(NB):
                    dve.wait_ge(s["zT_hi_ok"], NB * i + f + 1)
                    dve.tensor_tensor(zT_lo[:, f, :], ps[:, bank + f, :], zT_hi[:, f, :].bitcast(F32),
                                      ALU.subtract).then_inc(s["zT_lo_ok"], 1)

            def k_phase(i):
                def masked(j):
                    dve.wait_ge(s["k_exp"], NB * i + j + 1)
                    dve.scalar_tensor_tensor(out=ekTm[:, j, :], in0=ekT[:, j % 2, :], scalar=1.0, in1=mrow[:],
                                             op0=ALU.mult, op1=ALU.mult,
                                             accum_out=zs_new[:, 1, j:j + 1]).then_inc(s["k_masked"], 1)

                for j in range(NB):
                    n = NB * i + j + 1
                    dve.wait_ge(s["penb_ok"], n)
                    if j >= 2:
                        dve.wait_ge(s["k_exp"], NB * i + j - 1)
                    dve.wait_ge(s["k_ps"], n)
                    carry()
                    dve.tensor_tensor_reduce(kT[:, j % 2, :], ps[:, BB + j, :], pen_bias[:, j % 2, :], 1.0,
                                             kmax[:, j:j + 1], ALU.add, ALU.max,
                                             kmax_new[:, j:j + 1]).then_inc(s["k_max"], 1)
                    if j:
                        masked(j - 1)
                    dve.wait_ge(s["k_max"], n)
                    dve.tensor_scalar(nmax[:, j:j + 1], kmax_new[:, j:j + 1], -1.0, None, ALU.mult).then_inc(s["k_nmax"], 1)
                masked(NB - 1)

            def g_phase(i):
                for j in range(NB):
                    dve.wait_ge(s["k_alpha"], i + 1)
                    dve.wait_ge(s["g_ps"], NB * i + j + 1)
                    dve.scalar_tensor_tensor(out=g_acc[:, j, :], in0=g_acc[:, j, :], scalar=alpha[:, j:j + 1],
                                             in1=ps[:, A + j, :], op0=ALU.mult, op1=ALU.add).then_inc(s["g_ok"], 1)

            def q_tile(i, t, bank):
                n = NT * i + t + 1
                dve.wait_ge(s["q_ps"], n)
                if t >= 2:
                    dve.wait_ge(s["q_exp"], NT * i + t - 1)
                dve.tensor_tensor(qs[:, t % 2, :], ps[:, bank, :], bq_all[:], ALU.add).then_inc(s["q_sum"], 1)
                q_heads = qs[:, t % 2, :].rearrange("p (h d) -> p h d", h=H)
                dve.wait_ge(s["q_sum"], n)
                dve.tensor_reduce(qmax[:, t % 2, :], q_heads, AX_X, ALU.max).then_inc(s["q_max"], 1)
                dve.wait_ge(s["q_max"], n)
                dve.tensor_tensor(q_heads, q_heads, qmax[:, t % 2, :].unsqueeze(2).broadcast_to([P, H, DH]),
                                  ALU.subtract).then_inc(s["q_shift"], 1)

            def ek_low(i):
                for t in range(NT):
                    dve.wait_ge(s["ek_hi_ok"], NT * i + t + 1)
                    dve.tensor_tensor(ek_lo[:, t, :], ps[:, A + t, :], ek_hi[:, t, :].bitcast(F32),
                                      ALU.subtract).then_inc(s["ek_lo_ok"], 1)

            def phase1(i, first, left):
                k_phase(i)
                if not first:
                    g_phase(i - 1)
                dve.wait_ge(s["k_max"], NB * i + NB)
                dve.tensor_tensor(dmax[:], kmax[:], kmax_new[:], ALU.subtract).then_inc(s["k_shift"], 1)
                dve.wait_ge(s["k_shift"], i + 1)
                dve.tensor_copy(kmax[:], kmax_new[:]).then_inc(s["k_saved"], 1)
                dve.wait_ge(s["k_alpha"], i + 1)
                dve.wait_ge(s["k_masked"], NB * i + NB)
                dve.tensor_tensor(zs[:], zs[:], alpha[:].unsqueeze(1).broadcast_to([P, 2, NB]), ALU.mult).then_inc(s["zs_step"], 1)
                dve.wait_ge(s["zs_step"], 2 * i + 1)
                dve.tensor_tensor(zs[:], zs[:], zs_new[:], ALU.add).then_inc(s["zs_step"], 1)
                q_tile(i, 0, BB)
                q_tile(i, 1, BB + 1)
                if left:
                    q_tile(i, 2, BB + 2)
                    q_tile(i, 3, BB + 3)
                    zT_low(i + 1, BB)
                ek_low(i)
                if left:
                    penalty(i + 1)
                if left > 1 and not first:
                    x_stats(i + 2)

            def reset(b):
                if b:
                    dve.wait_ge(s["k_saved"], NC * b)
                    dve.wait_ge(s["att_step"], 6 * b)
                    dve.wait_ge(s["embT_ps"], 1)
                dve.memset(kmax[:], -LEAST)
                dve.memset(zs[:], 0.0)
                dve.memset(g_acc[:], 0.0).then_inc(s["reset_ok"], 1)
                dve.wait_ge(s["reset_ok"], b + 1)

            def condition_scale():
                dve.wait_ge(s["embT_ps"], 1)
                for b in range(B):
                    dve.tensor_tensor(emb_cols[:, b, :], ps[:, BB + 3, 0:2 * B * NB].rearrange("p (c b) -> p b c", b=B)[:, b, :],
                                      cols[:, BEMB:BEMB + 2 * NB], ALU.add).then_inc(s["embc_ok"], 1)
                dve.wait_ge(s["embc_ok"], B)
                for b in range(B):
                    for k, w in ((0, LN2W), (1, LN2B)):
                        dve.scalar_tensor_tensor(out=ab[:, b, k, :], in0=emb_cols[:, b, 0:NB], scalar=1.0,
                                                 in1=cols[:, w:w + NB], op0=ALU.add, op1=ALU.mult).then_inc(s["ab_step"], 1)
                    dve.wait_ge(s["ab_step"], 3 * b + 2)
                    dve.tensor_tensor(ab[:, b, 1, :], ab[:, b, 1, :], emb_cols[:, b, NB:2 * NB],
                                      ALU.add).then_inc(s["ab_step"], 1)

            def att_blocks(b):
                dve.wait_ge(s["zs_step"], 2 * NC * (b + 1))
                dve.reciprocal(rz[:], zs[:, 0, :]).then_inc(s["rz_ok"], 1)
                rows = [slice(DH * h, DH * h + DH) for h in range(2)]
                part = [pen[r, 0:NB * DH].rearrange("p (q d) -> p q d", q=NB) for r in rows]

                def of_head(t, h):
                    return t[rows[h], :].rearrange("p (q h d) -> p q h d", q=NB, h=2)[:, :, h, :]

                for h, r in enumerate(rows):
                    dve.tensor_tensor(part[h], of_head(bv_all, h), zs[r, 1, :].unsqueeze(2).broadcast_to([DH, NB, DH]),
                                      ALU.mult).then_inc(s["att_step"], 1)
                dve.wait_ge(s["rz_ok"], b + 1)
                dve.wait_ge(s["att_ps"], b + 1)
                dve.wait_ge(s["att_step"], 6 * b + 2)
                for h in range(2):
                    dve.tensor_tensor(part[h], part[h], of_head(ps[:, A + 1, :], h), ALU.add).then_inc(s["att_step"], 1)
                dve.wait_ge(s["att_step"], 6 * b + 4)
                for h, r in enumerate(rows):
                    dve.tensor_tensor(att[r, :, DH * h:DH * h + DH], part[h],
                                      rz[r, :].unsqueeze(2).broadcast_to([DH, NB, DH]), ALU.mult).then_inc(s["att_step"], 1)

            def y_tile(g, t):
                n = NT * g + t + 1
                tile = ps[:, A + 2 * (t % 2):A + 2 * (t % 2) + 2, :].rearrange("p k (q c) -> p (k q) c", c=YS)
                rec_t = rec[:, t % 2, :].rearrange("p (q h) -> p q h", h=2)
                dve.wait_ge(s["y_ps"], n)
                if n > 2:
                    dve.wait_ge(s["y_ok"], n - 2)
                dve.reciprocal(rec_t, tile[:, :, P:YW]).then_inc(s["y_rec"], 1)
                dve.wait_ge(s["y_rec"], n)
                dve.tensor_tensor(y[g % NC][:, t, :].rearrange("p (q h d) -> p q h d", q=NB, h=2),
                                  tile[:, :, 0:P].rearrange("p q (h d) -> p q h d", h=2),
                                  rec_t.unsqueeze(3).broadcast_to([P, NB, 2, DH]), ALU.mult).then_inc(s["y_ok"], 1)

            def y_tile_stats(g, t):
                dve.wait_ge(s["y_ok"], NT * g + t + 1)
                tile_stats(y[g % NC], yst[g % 2], t, "ystat")

            def y_finish(g, between=lambda k: None):
                finish_stats(yst[g % 2], "ystat", STAT_STEPS * g, "y_norm", between)

            def y_with_stats(g):
                for t in range(NT + 1):
                    if t < NT:
                        y_tile(g, t)
                    if t:
                        y_tile_stats(g, t - 1)

            def every(steps, do):
                return lambda k: do(k // steps) if k % steps == 0 and k // steps < 4 else None

            def silu_block(g, f):
                dve.wait_ge(s["th_ok"], NB * g + f + 1)
                dve.scalar_tensor_tensor(out=th[f], in0=th[f], scalar=1.0, in1=u[f],
                                         op0=ALU.add, op1=ALU.mult).then_inc(s["h_ok"], 1)

            def out_tile(g, t):
                dve.wait_ge(s["o_ps"], NT * g + t + 1)
                dve.wait_ge(s["res_b"], NT * g + t + 1)
                dve.tensor_tensor(res[:, t, :], ps[:, BB + t, :], res[:, t, :], ALU.add).then_inc(s["o_ok"], 1)

            dve.memset(ones, 1.0).then_inc(s["ones_ok"], 1)
            dve.memset(att[:], 0.0).then_inc(s["att0"], 1)
            dve.wait_ge(s["att0"], 1)
            dve.memset(att[0:DH, :, P:P + 1], 1.0).then_inc(s["att0"], 1)
            dve.memset(att[DH:P, :, P + 1:P + 2], 1.0).then_inc(s["att0"], 1)
            dve.wait_ge(s["vec_ps"], 1)
            dve.tensor_copy(cols[:, 0:FIRST], ps[:, 0, 0:FIRST]).then_inc(s["cols_ok"], 1)
            dve.wait_ge(s["cols_ok"], 1)
            dve.wait_ge(s["ones_ok"], 1)
            for f in range(NB):
                dve.tensor_scalar(lnb_wide[:, f, :], ones, cols[:, LNB + f:LNB + f + 1], None,
                                  ALU.mult).then_inc(s["lnb_ok"], 1)
            x_stats(0)

            def low_weights(raw, hi, lo, got, ok):
                for f in range(NB):
                    dve.wait_ge(s[got], f + 1)
                    dve.scalar_tensor_tensor(out=lo[:, f, :], in0=raw[:, f, :], scalar=cols[:, LNW + f:LNW + f + 1],
                                             in1=hi[:, f, :].bitcast(F32), op0=ALU.mult, op1=ALU.subtract).then_inc(s[ok], 1)

            dve.wait_ge(s["bias_ps"], 1)
            dve.tensor_copy(bk_rows, ps[:, 1, :]).then_inc(s["bk_row_ok"], 1)
            low_weights(wk_raw, wk_hi, wk_lo, "wk_hi_ok", "wk_lo_ok")
            dve.wait_ge(s["vec_ps"], 2)
            dve.tensor_copy(cols[:, FIRST:ROWS], ps[:, 0, 0:ROWS - FIRST]).then_inc(s["cols_ok"], 1)
            dve.wait_ge(s["cols_ok"], 2)
            dve.wait_ge(s["bk_ps"], 1)
            dve.tensor_tensor(cols[:, BK:BK + NB], cols[:, BK:BK + NB],
                              ps[:, 3, :].rearrange("p (j c) -> p j c", j=NB)[:, :, 0], ALU.add).then_inc(s["bk_ok"], 1)
            penalty(0)
            zT_low(0, BB)
            low_weights(wq_raw, wq_hi, wq_lo, "wq_hi_ok", "wq_lo_ok")
            dve.wait_ge(s["bias_in"], 48)
            dve.wait_ge(s["bias_ps"], 3)
            dve.tensor_tensor(bq_all[:], bq_all[:], ps[:, 2, :], ALU.add).then_inc(s["bq_ok"], 1)
            dve.tensor_tensor(bv_all[:], bv_all[:], ps[:, 0, :], ALU.add).then_inc(s["bq_ok"], 1)
            dve.wait_ge(s["bq_ok"], 2)

            reset(0)
            x_stats(1)

            for b in range(B):
                i0 = b * NC
                phase1(i0, True, 2)
                x_stats(i0 + 2)
                if b == 0:
                    for f in range(NB):
                        dve.wait_ge(s["wo_hi_ok"], f + 1)
                        dve.scalar_tensor_tensor(out=wo_lo[:, f, :], in0=wo_raw[:, f, :], scalar=0.5,
                                                 in1=wo_hi[:, f, :].bitcast(F32), op0=ALU.mult,
                                                 op1=ALU.subtract).then_inc(s["wo_lo_ok"], 1)
                    dve.wait_ge(s["sig_ok"], 1)
                    dve.scalar_tensor_tensor(out=semb_t[:], in0=semb_t[:], scalar=1.0, in1=cols[:, COND:ROWS],
                                             op0=ALU.add, op1=ALU.mult).then_inc(s["semb_step"], 1)
                    dve.wait_ge(s["semb_step"], 1)
                    dve.tensor_scalar(semb[:], semb_t[:].rearrange("p (b t) -> p t b", b=B), 0.5, None,
                                      ALU.mult).then_inc(s["semb_ok"], 1)
                with dve.Fori(1, NC - 2) as c:
                    phase1(i0 + c, False, 2)
                phase1(i0 + NC - 2, False, 1)
                phase1(i0 + NC - 1, False, 0)
                g_phase(i0 + NC - 1)
                q_tile(i0 + NC - 1, 2, BB + 3)
                if b == 0:
                    dve.wait_ge(s["emb_ps"], 1)
                    dve.tensor_copy(emb_rows[:, 0:D], ps[0:B, A, :]).then_inc(s["emb_ok"], 1)
                q_tile(i0 + NC - 1, 3, A + 3)
                att_blocks(b)

                y_with_stats(i0)
                y_finish(i0)
                if b == 0:
                    dve.wait_ge(s["emb_ps"], 2)
                    dve.tensor_copy(emb_rows[:, D:2 * D], ps[0:B, A, :]).then_inc(s["emb_ok"], 1)
                y_with_stats(i0 + 1)
                if b == 0:
                    condition_scale()
                y_finish(i0 + 1)
                for t in range(NT):
                    y_tile(i0 + 2, t)
                for t in range(NT):
                    silu_block(i0, t)
                for t in range(NT):
                    y_tile_stats(i0 + 2, t)
                y_finish(i0 + 2, every(3, lambda t: silu_block(i0 + 1, t)))
                for t in range(NT):
                    out_tile(i0, t)
                y_with_stats(i0 + 3)
                y_finish(i0 + 3, every(3, lambda t: silu_block(i0 + 2, t)))
                for t in range(NT):
                    out_tile(i0 + 1, t)
                if b + 1 < B:
                    x_stats(i0 + NC)
                for t in range(NT):
                    silu_block(i0 + 3, t)
                for t in range(NT):
                    out_tile(i0 + 2, t)
                if b + 1 < B:
                    penalty(i0 + NC)
                    zT_low(i0 + NC, A)
                    reset(b + 1)
                    x_stats(i0 + NC + 1)
                for t in range(NT):
                    out_tile(i0 + 3, t)

        @block.tensor
        def _(pe):
            def split_product(o, a, bb, start, stop):
                pe.matmul(o, a[0], bb[0], start=start, stop=False)
                pe.matmul(o, a[0], bb[1], start=False, stop=False)
                return pe.matmul(o, a[1], bb[0], start=False, stop=stop)

            def turn(o, i):
                return pe.transpose(o, i, ident[0:i.shape[0], 0:i.shape[0]])

            def turn_z(i, bank, free):
                pe.wait_ge(s["z_ok"], NT * i + NT)
                for f in range(NB):
                    free(f)
                    for t in range(NT):
                        last = turn(blk(ps[:, bank + f, :], t), blk(z[:, t, :], f))
                    last.then_inc(s["zT_ps"], 1)

            def products_k(i, free):
                for j in range(NB):
                    free(j)
                    for f in range(NB):
                        if j == 0:
                            pe.wait_ge(s["zT_lo_ok"], NB * i + f + 1)
                        last = split_product(ps[:, BB + j, :], (blk(wk_hi[:, f, :], j), blk(wk_lo[:, f, :], j)),
                                             (zT_hi[:, f, :], zT_lo[:, f, :]), f == 0, f == NB - 1)
                    last.then_inc(s["k_ps"], 1)

            def products_q(i, t, bank):
                for f in range(NB):
                    last = split_product(ps[:, bank, :], (blk(zT_hi[:, f, :], t), blk(zT_lo[:, f, :], t)),
                                         (wq_hi[:, f, :], wq_lo[:, f, :]), f == 0, f == NB - 1)
                last.then_inc(s["q_ps"], 1)

            def products_all_q(i):
                for t in range(NT):
                    pe.wait_ge(s["k_max"], NB * i + t + 1)
                    products_q(i, t, BB + t)

            def turn_k(i):
                pe.wait_ge(s["k_masked"], NB * i + NB)
                for t in range(NT):
                    for j in range(NB):
                        last = turn(blk(ps[:, A + t, :], j), blk(ekTm[:, j, :], t))
                    last.then_inc(s["ek_ps"], 1)

            def products_g(i):
                for t in range(NT):
                    pe.wait_ge(s["z_lo_ok"], NT * i + t + 1)
                    for j in range(NB):
                        if t == 0:
                            pe.wait_ge(s["ek_lo_ok"], NT * i + j + 1)
                        last = split_product(ps[:, A + j, :], (blk(ek_hi[:, t, :], j), blk(ek_lo[:, t, :], j)),
                                             (z_hi[:, t, :], z_lo[:, t, :]), t == 0, t == NT - 1)
                        if t == NT - 1:
                            last.then_inc(s["g_ps"], 1)

            def turn_q(g, free):
                pe.wait_ge(s["q_exp"], NT * g + NT)
                for j in range(NB):
                    free(j)
                    for t in range(NT):
                        last = turn(blk(ps[:, BB + j, :], t), blk(eq[:, (g % NC) * NT + t, :], j))
                    last.then_inc(s["eqT_ps"], 1)

            def products_y(g):
                pe.wait_ge(s["eqT_ok"], NB * g + NB)
                for t in range(NT):
                    if NT * g + t > 1:
                        pe.wait_ge(s["y_ok"], NT * g + t - 1)
                    for q in range(NB):
                        bank, at = A + 2 * (t % 2) + q // 2, (q % 2) * YS
                        last = pe.matmul(ps[:, bank, at:at + YW], blk(eqT(g)[:, q, :], t), att[:, q, :], start=True, stop=True)
                    last.then_inc(s["y_ps"], 1)

            def turn_y(g, free):
                pe.wait_ge(s["yn_ok"], NT * g + NT)
                for f in range(NB):
                    free(f)
                    for t in range(NT):
                        last = turn(blk(ps[:, BB + f, :], t), blk(y[g % NC][:, t, :], f))
                    last.then_inc(s["ynT_ps"], 1)

            def products_out(g, free):
                for t in range(NT):
                    free(t)
                    for f in range(NB):
                        if t == 0:
                            pe.wait_ge(s["h_lo_ok"], NB * g + f + 1)
                        hi, lo = hT[g % 2]
                        last = split_product(ps[:, BB + t, :], (blk(hi[:, f, :], t), blk(lo[:, f, :], t)),
                                             (wo_hi[:, f, :], wo_lo[:, f, :]), f == 0, f == NB - 1)
                    last.then_inc(s["o_ps"], 1)

            def condition(h, bank):
                for t in range(NTE):
                    n = NTE * h + t
                    pe.wait_ge(wemb_in[n], 16)
                    last = pe.matmul(ps[0:B, bank, :], semb[:, t, :], wemb[n % NW], start=(t == 0), stop=(t == NTE - 1))
                last.then_inc(s["emb_ps"], 1)

            def ready(name, n):
                return lambda k: pe.wait_ge(s[name], n + k)

            pe.wait_ge(s["ident_ok"], 1)
            pe.wait_ge(s["ln_in"], 2 * 16)
            turn(ps[:, 0, 0:FIRST], ln_rows[:]).then_inc(s["vec_ps"], 1)
            pe.wait_ge(s["lnb_ok"], NB)
            for bank, raw, got in ((1, wk_raw, "wk_in"), (2, wq_raw, "wq_in")):
                pe.wait_ge(s[got], 16)
                for f in range(NB):
                    last = pe.matmul(ps[:, bank, :], lnb_wide[:, f, :], raw[:, f, :], start=(f == 0), stop=(f == NB - 1))
                last.then_inc(s["bias_ps"], 1)
            pe.wait_ge(s["bk_row_ok"], 1)
            for j in range(NB):
                last = turn(blk(ps[:, 3, :], j), blk(bk_rows, j))
            last.then_inc(s["bk_ps"], 1)
            turn_z(0, BB, lambda f: None)
            pe.wait_ge(s["vec_in"], 5 * 16)
            pe.wait_ge(s["cols_ok"], 1)
            turn(ps[:, 0, 0:ROWS - FIRST], vec_rows[:]).then_inc(s["vec_ps"], 1)
            pe.wait_ge(s["cols_ok"], 2)
            pe.wait_ge(s["wv_in"], 16)
            for f in range(NB):
                last = pe.matmul(ps[:, 0, :], lnb_wide[:, f, :], wv_raw[:, f, :], start=(f == 0), stop=(f == NB - 1))
            last.then_inc(s["bias_ps"], 1)
            pe.wait_ge(s["wk_lo_ok"], NB)

            for b in range(B):
                i0 = b * NC
                products_k(i0, ready("o_ok", NT * (i0 - 1) + 1) if b else lambda j: None)
                if b == 0:
                    pe.wait_ge(s["wq_lo_ok"], NB)
                products_all_q(i0)
                turn_z(i0 + 1, BB, ready("q_sum", NT * i0 + 1))
                if b == 0:
                    pe.wait_ge(s["bq_ok"], 2)
                turn_k(i0)
                with pe.Fori(1, NC - 1) as c:
                    i = i0 + c
                    products_k(i, lambda j: None)
                    products_g(i - 1)
                    products_all_q(i)
                    pe.wait_ge(s["g_ok"], NB * i)
                    turn_z(i + 1, BB, ready("q_sum", NT * i + 1))
                    turn_k(i)
                i = i0 + NC - 1
                products_k(i, lambda j: None)
                products_g(i - 1)
                for t in range(2):
                    pe.wait_ge(s["k_max"], NB * i + t + 1)
                    products_q(i, t, BB + t)
                pe.wait_ge(s["g_ok"], NB * i)
                turn_k(i)
                pe.wait_ge(s["k_max"], NB * i + NB)
                turn_q(i0, lambda j: pe.wait_ge(s["q_sum"], NT * i + j + 1) if j < 2 else None)
                products_g(i)
                pe.wait_ge(s["eqT_ok"], NB * i0 + NB)
                products_q(i, 2, BB + 3)

                pe.wait_ge(s["g_ok"], NB * i + NB)
                for f in range(NB):
                    if f == NB - 1:
                        pe.wait_ge(s["q_sum"], NT * i + 3)
                    for j in range(NB):
                        last = turn(blk(ps[:, BB + f, :], j), blk(g_acc[:, j, :], f))
                    last.then_inc(s["gT_ps"], 1)
                if b == 0:
                    pe.wait_ge(s["semb_ok"], 1)
                    condition(0, A)
                    pe.wait_ge(s["wv_ok"], NB)
                products_q(i, 3, A + 3)
                pe.wait_ge(s["gT_ok"], NB * b + NB)
                for q in range(NB):
                    for f in range(NB):
                        last = pe.matmul(blk(ps[:, A + 1, :], q), blk(gT[:, f, :], q), blk(wv_sc[:, f, :], q),
                                         start=(f == 0), stop=(f == NB - 1))
                last.then_inc(s["att_ps"], 1)
                turn_q(i0 + 1, lambda j: None)
                if b == 0:
                    pe.wait_ge(s["emb_ok"], 1)
                pe.wait_ge(s["q_sum"], NT * i + NT)
                pe.wait_ge(s["att_step"], 6 * b + 6)
                products_y(i0)
                if b == 0:
                    pe.wait_ge(s["y_ok"], NT - 1)
                    condition(1, A)
                    pe.wait_ge(s["emb_ok"], 2)
                products_y(i0 + 1)
                if b == 0:
                    for k in range(2 * NB):
                        last = turn(ps[:, BB + 3, B * k:B * k + B], blk(emb_rows, k))
                    last.then_inc(s["embT_ps"], 1)
                    turn_q(i0 + 2, lambda j: pe.wait_ge(s["embc_ok"], B) if j == 3 else None)
                else:
                    turn_q(i0 + 2, lambda j: None)
                turn_y(i0, ready("eqT_ok", NB * (i0 + 2) + 1))
                products_y(i0 + 2)
                turn_q(i0 + 3, ready("u_ok", NB * i0 + 1))
                turn_y(i0 + 1, ready("eqT_ok", NB * (i0 + 3) + 1))
                products_out(i0, ready("u_ok", NB * (i0 + 1) + 1))
                turn_y(i0 + 2, ready("o_ok", NT * i0 + 1))
                products_y(i0 + 3)
                products_out(i0 + 1, ready("u_ok", NB * (i0 + 2) + 1))
                turn_y(i0 + 3, ready("o_ok", NT * (i0 + 1) + 1))
                products_out(i0 + 2, ready("u_ok", NB * (i0 + 3) + 1))
                if b + 1 < B:
                    turn_z(i0 + NC, A, lambda f: None)
                products_out(i0 + NC - 1, ready("o_ok", NT * (i0 + NC - 2) + 1))


_INS = ["x", "cond_2048", "mask_BxSx1_fk1"] + ["L0_cond_" + n for n in (
    "ln_w", "ln_b", "Wq", "bq", "Wk", "bk", "Wv", "bv", "W_emb", "b_emb", "ln2_w", "ln2_b", "W_out", "b_out")]


def kernel(**inputs):
    import numpy as _np
    import concourse.bacc as _bacc
    from concourse import mybir as _mybir
    from concourse.bass_utils import run_bass_kernel_spmd as _run

    nc = _bacc.Bacc("TRN2", target_bir_lowering=False, num_devices=1)
    arrays, args = {}, []
    for name in _INS:
        a = _np.ascontiguousarray(inputs[name])
        arrays[f"in_{name}_dram"] = a
        args.append(nc.dram_tensor(f"in_{name}_dram", a.shape, _mybir.dt.from_np(a.dtype), kind="ExternalInput").ap())
    shape = _np.shape(inputs["x"])
    args.append(nc.dram_tensor("out_dram", shape, _mybir.dt.float32, kind="ExternalOutput").ap())
    cond_linear_attention(nc, *args)
    r = _run(nc, [arrays], core_ids=[0])
    return r.results[0]["out_dram"]
```

```python
from contextlib import ExitStack

import concourse.bass as bass
from concourse import mybir

F32 = mybir.dt.float32
F32R = mybir.dt.float32r
U32 = mybir.dt.uint32
I32 = mybir.dt.int32
ALU = mybir.AluOpType
ACT = mybir.ActivationFunctionType
AX_X = mybir.AxisListType.X

P = 128
EPS = 1e-5
MASK_PENALTY = 1e6
RSQRT_SEED = 0x5F3759DF
LEAST = 3.0e38
STAT_STEPS = 20


def cond_linear_attention(nc, x, cond, mask, ln_w, ln_b, wq, bq, wk, bk, wv, bv, w_emb, b_emb,
                          ln2_w, ln2_b, w_out, b_out, out):
    B, S, D = x.shape
    TE = cond.shape[1]
    DH = 64
    NB = D // P
    C = 4 * P
    NT = C // P
    NC = S // C
    NTE = TE // P
    H = D // DH
    YW = P + 2
    YS = 2 * P
    assert NT == 4 and NB == 4 and H == 8 and B == 2 and NC == 4 and NTE == 8

    x_tok = x.rearrange("b (n p) d -> p (b n) d", p=P)
    out_tok = out.rearrange("b (n p) d -> p (b n) d", p=P)
    mask_row = mask.rearrange("b s o -> o (b s)")

    LNW, LNB, BK, LN2W, LN2B, BEMB = 0, NB, 2 * NB, 3 * NB, 4 * NB, 5 * NB
    COND = BEMB + 2 * NB
    ROWS = COND + B * NTE
    FIRST = BK

    with ExitStack() as ctx:
        def sb(name, shape, dt=F32):
            return ctx.enter_context(nc.sbuf_tensor(name, shape, dt))

        def sem(name):
            return ctx.enter_context(nc.semaphore(name))

        ps = ctx.enter_context(nc.psum_tensor("ps", [P, 8, 512], F32))
        A, BB = 0, 4

        wk_hi, wk_lo = sb("wk_hi", [P, NB, D], F32R), sb("wk_lo", [P, NB, D], F32R)
        wq_hi, wq_lo = sb("wq_hi", [P, NB, D], F32R), sb("wq_lo", [P, NB, D], F32R)
        wo_hi, wo_lo = sb("wo_hi", [P, NB, D], F32R), sb("wo_lo", [P, NB, D], F32R)
        wv_sc = sb("wv_sc", [P, NB, D])
        bq_all, bv_all, bo_all = (sb(n, [P, D]) for n in ("bq_all", "bv_all", "bo_all"))
        ident = sb("ident", [P, P])
        ones = sb("ones", [P, P])
        vec_rows = sb("vec_rows", [ROWS - FIRST, P])
        cols = sb("cols", [P, ROWS])
        semb = sb("semb", [P, NTE, B])
        semb_t = sb("semb_t", [P, B * NTE])
        emb_cols = sb("emb_cols", [P, B, 2 * NB])
        ab = sb("ab", [P, B, 2, NB])

        x_in = sb("x_in", [P, NT, D])
        z = sb("z", [P, NT, D])
        z_hi, z_lo = sb("z_hi", [P, NT, D], F32R), sb("z_lo", [P, NT, D], F32R)
        zT_hi, zT_lo = sb("zT_hi", [P, NB, C], F32R), sb("zT_lo", [P, NB, C], F32R)
        mrow, pen = sb("mrow", [P, C]), sb("pen", [P, C])
        pen_bias = sb("pen_bias", [P, 2, C])
        kT = sb("kT", [P, 2, C])
        ekT = sb("ekT", [P, 2, C])
        ekTm = sb("ekTm", [P, NB, C])
        ek_hi, ek_lo = sb("ek_hi", [P, NT, D], F32R), sb("ek_lo", [P, NT, D], F32R)
        qs = sb("qs", [P, 2, D])
        qmax = sb("qmax", [P, 2, H])
        eq = sb("eq", [P, NC * NT, D])
        g_acc = sb("g_acc", [P, NB, D])
        att = sb("att", [P, NB, YW])
        kmax, kmax_new, nmax, dmax, alpha = (sb(n, [P, NB]) for n in ("kmax", "kmax_new", "nmax", "dmax", "alpha"))
        zs, zs_new = sb("zs", [P, 2, NB]), sb("zs_new", [P, 2, NB])
        rz = sb("rz", [P, NB])

        def stat_tiles(n):
            return {"raw": sb(n + "_raw", [P, NT, 6]), "mv": sb(n + "_mv", [P, NT, 2]),
                    "v": sb(n + "_v", [P, NT]), "bits": sb(n + "_bits", [P, NT], U32),
                    "y": sb(n + "_y", [P, NT], I32), "a": sb(n + "_a", [P, NT]),
                    "b": sb(n + "_b", [P, NT]), "r": sb(n + "_r", [P, NT]),
                    "shift": sb(n + "_shift", [P, NT])}

        xst, yst = stat_tiles("xst"), [stat_tiles("yst0"), stat_tiles("yst1")]
        go = sb("go", [P, 1])

        res = sb("res", [P, NT, D])
        rec = sb("rec", [P, 2, H])
        gT = res[:]

        def eqT(g):
            return g_acc[:] if g == NC + 1 else z[:]

        y = [ekTm[:], x_in[:], ekTm[:], ekTm[:]]
        hT = [(ek_hi[:], ek_lo[:]), (z_hi[:], z_lo[:])]
        u = [kT[:, 0, :], kT[:, 1, :], qs[:, 0, :], qs[:, 1, :]]
        th = [ekT[:, 0, :], ekT[:, 1, :], pen_bias[:, 0, :], pen_bias[:, 1, :]]
        wemb = [kT[:, 0, :], kT[:, 1, :], ekT[:, 0, :], ekT[:, 1, :], pen_bias[:, 0, :], pen_bias[:, 1, :]] + \
            [x_in[:, t, :] for t in range(NT)]
        NW = len(wemb)
        emb_rows = g_acc[0:B, 0:2, :].rearrange("b k d -> b (k d)")
        wk_raw, wq_raw, wv_raw, wo_raw = g_acc[:], ekTm[:], wv_sc[:], res[:]
        ln_rows = eq[0:FIRST, 0, 0:P]
        lnb_wide = qs[:, 1, :].rearrange("p (c d) -> p c d", c=NB)
        bk_rows = qs[:, 0, :]
        lnb_wq, lnb_wv = eq[:, 1, :], res[:, 0, :]

        names = """x0_ok table_ok ln_in vec_in wk_in wq_in wv_in wo_in bias_in ident0 ident_ok ones_ok vec_ps cols_ok
            lnb_ok lnb_wq_step lnb_wv_step bias_ps bk_row_ok bk_ps bk_ok bq_ok bv_ok wq_sc_ok g_zero wk_hi_ok wq_hi_ok wv_ok wo_hi_ok wk_lo_ok wq_lo_ok wo_lo_ok
            sig_ok semb_step semb_ok emb_ps emb_ok embT_ps embc_ok ab_step att0
            x_ok mask_ok pen_ok penb_ok xstat x_norm z_ok zT_ps zT_hi_ok zT_lo_ok z_hi_ok z_lo_ok
            k_ps k_max k_nmax k_exp k_masked k_shift k_saved k_alpha zs_step
            ek_ps ek_hi_ok ek_lo_ok g_ps g_ok q_ps q_sum q_max q_shift q_exp reset_ok
            rz_ok gT_ps gT_ok att_ps att_step
            eqT_ps eqT_ok y_ps y_rec y_ok ystat y_norm yn_ok ynT_ps u_ok th_ok h_ok h_hi_ok h_lo_ok
            o_ps o_ok res_b""".split()
        s = {n: sem(n) for n in names}
        res_in = [sem(f"res_in{t}") for t in range(NT)]
        stored = [sem(f"stored{t}") for t in range(NT)]
        wemb_in = [sem(f"wemb_in{n}") for n in range(2 * NTE)]

        def blk(t, n):
            return t[:, n * P:(n + 1) * P]

        block = ctx.enter_context(nc.Block())

        @block.sync
        def _(sp):
            def load_x(i):
                sp.dma_start(x_in[:], x_tok[:, bass.ts(i, NT), :]).then_inc(s["x_ok"], 16)

            def load_mask(i):
                sp.dma_start(mrow[:], mask_row[0:1, bass.ts(i, C)].broadcast_to([P, C])).then_inc(s["mask_ok"], 16)

            def load_res(g, t):
                sp.dma_start(res[:, t, :], x_tok[:, NT * g + t, :]).then_inc(res_in[t], 16)

            def load_wemb(first, end):
                for n in range(first, end):
                    h, t = n // NTE, n % NTE
                    sp.dma_start(wemb[n % NW], w_emb[t * P:(t + 1) * P, h * D:(h + 1) * D]).then_inc(wemb_in[n], 16)

            def next_x(i):
                sp.wait_ge(s["z_ok"], NT * i + NT)
                load_x(i + 1)

            def next_mask(i):
                sp.wait_ge(s["k_masked"], NB * i + NB)
                load_mask(i + 1)

            for v, at in ((ln_w, LNW), (ln_b, LNB)):
                sp.dma_start(ln_rows[at:at + NB, :], v.rearrange("(c p) -> c p", p=P)).then_inc(s["ln_in"], 16)
            for v, at in ((bk, BK), (ln2_w, LN2W), (ln2_b, LN2B), (b_emb, BEMB)):
                n = v.shape[0] // P
                sp.dma_start(vec_rows[at - FIRST:at - FIRST + n, :], v.rearrange("(c p) -> c p", p=P)).then_inc(s["vec_in"], 16)
            sp.dma_start(vec_rows[COND - FIRST:, :], cond.rearrange("b (t p) -> (b t) p", p=P)).then_inc(s["vec_in"], 16)
            load_mask(0)
            for v, to in ((bq, bq_all), (bv, bv_all), (b_out, bo_all)):
                sp.dma_start(to[:], v.rearrange("(o d) -> o d", o=1).broadcast_to([P, D])).then_inc(s["bias_in"], 16)
            sp.dma_start(wo_raw, w_out.rearrange("(c p) n -> p c n", p=P)).then_inc(s["wo_in"], 16)
            for b in range(B):
                i0 = b * NC
                if b == 0:
                    next_x(0)
                next_mask(i0)
                with sp.Fori(1, NC - 1) as c:
                    next_x(i0 + c)
                    next_mask(i0 + c)
                if b == 0:
                    sp.wait_ge(s["k_masked"], NB * NC)
                    sp.wait_ge(s["z_ok"], NT * NC)
                    load_mask(NC)
                    load_wemb(0, NW)
                    sp.wait_ge(s["emb_ps"], 1)
                    load_wemb(NW, 2 * NTE)
                sp.wait_ge(s["att_ps"], b + 1)
                for t in range(NT):
                    load_res(i0, t)
                for g in range(i0, i0 + NC):
                    for t in range(NT):
                        sp.wait_ge(s["o_ok"], NT * g + t + 1)
                        sp.dma_start(out_tok[:, NT * g + t, :], res[:, t, :]).then_inc(stored[t], 16)
                        if g + 1 < i0 + NC:
                            if t:
                                sp.wait_ge(stored[t - 1], 16 * g + 16)
                                load_res(g + 1, t - 1)
                    if g + 1 < i0 + NC:
                        sp.wait_ge(stored[NT - 1], 16 * g + 16)
                        load_res(g + 1, NT - 1)
                    if g == i0 and b + 1 < B:
                        sp.wait_ge(s["ynT_ps"], NB * (g + 2))
                        load_x(i0 + NC)
                    if g == i0 + 2 and b + 1 < B:
                        next_x(i0 + NC)
            for t in range(NT):
                sp.wait_ge(stored[t], 16 * B * NC)

        @block.scalar
        def _(act):
            def copy(o, i, done, scale=1.0):
                act.activation(o, i, ACT.Copy, scale=scale).then_inc(s[done], 1)

            def ln_weight(f):
                return cols[:, LNW + f:LNW + f + 1]

            for half in range(2):
                r = slice(half * NT // 2, (half + 1) * NT // 2)
                act.dma_start(x_in[:, r, :], x_tok[:, r, :]).then_inc(s[("x0_ok", "x_ok")[half]], 16)
            for w, raw, done in ((wk, wk_raw, "wk_in"), (wq, wq_raw, "wq_in"), (wv, wv_raw, "wv_in")):
                act.dma_start(raw, w.rearrange("(c p) n -> p c n", p=P)).then_inc(s[done], 16)

            def normalise_x(i, z_read=False):
                act.wait_ge(s["x_norm"], i + 1)
                if z_read:
                    act.wait_ge(s["z_hi_ok"], NT * i)
                for t in range(NT):
                    if z_read:
                        act.wait_ge(s["z_lo_ok"], NT * (i - 1) + t + 1)
                    act.activation(z[:, t, :], x_in[:, t, :], ACT.Identity, bias=xst["shift"][:, t:t + 1],
                                   scale=xst["r"][:, t:t + 1]).then_inc(s["z_ok"], 1)

            def zT_high(i, bank):
                for f in range(NB):
                    act.wait_ge(s["zT_ps"], NB * i + f + 1)
                    copy(zT_hi[:, f, :], ps[:, bank + f, :], "zT_hi_ok")

            def z_high(i):
                for t in range(NT):
                    act.wait_ge(s["z_ok"], NT * i + t + 1)
                    copy(z_hi[:, t, :], z[:, t, :], "z_hi_ok")

            def pen_with_bias(i, j):
                if j < 2:
                    act.wait_ge(s["pen_ok"], i + 1)
                else:
                    act.wait_ge(s["k_max"], NB * i + j - 1)
                act.activation(pen_bias[:, j % 2, :], pen[:], ACT.Identity,
                               bias=cols[:, BK + j:BK + j + 1]).then_inc(s["penb_ok"], 1)

            def exponentials_k(i, between=lambda: None):
                def exp_k(j):
                    act.wait_ge(s["k_nmax"], NB * i + j + 1)
                    if j >= 2:
                        act.wait_ge(s["k_masked"], NB * i + j - 1)
                    act.activation(ekT[:, j % 2, :], kT[:, j % 2, :], ACT.Exp, bias=nmax[:, j:j + 1],
                                   accum_out=zs_new[:, 0, j:j + 1]).then_inc(s["k_exp"], 1)

                exp_k(0)
                pen_with_bias(i, 2)
                exp_k(1)
                pen_with_bias(i, 3)
                between()
                exp_k(2)
                exp_k(3)

            def exp_q(i, c, t):
                act.wait_ge(s["q_shift"], NT * i + t + 1)
                to = eq[:, c * NT + t, :] if isinstance(c, int) else \
                    eq[:, bass.ds(c * NT + t, 1), :].rearrange("p o d -> p (o d)")
                act.activation(to, qs[:, t % 2, :], ACT.Exp).then_inc(s["q_exp"], 1)

            def ek_high(i):
                for t in range(NT):
                    act.wait_ge(s["ek_ps"], NT * i + t + 1)
                    copy(ek_hi[:, t, :], ps[:, A + t, :], "ek_hi_ok")

            def phase1(i, c, first, last):
                if first:
                    exponentials_k(i, lambda: z_high(i))
                else:
                    pen_with_bias(i, 0)
                    pen_with_bias(i, 1)
                    exponentials_k(i)
                    act.wait_ge(s["g_ps"], NB * i)
                    z_high(i)
                act.wait_ge(s["k_shift"], i + 1)
                act.activation(alpha[:], dmax[:], ACT.Exp).then_inc(s["k_alpha"], 1)
                if first:
                    normalise_x(i + 1, z_read=True)
                exp_q(i, c, 0)
                if last:
                    ek_high(i)
                    exp_q(i, c, 1)
                else:
                    if not first:
                        normalise_x(i + 1, z_read=True)
                    exp_q(i, c, 1)
                    exp_q(i, c, 2)
                    zT_high(i + 1, BB)
                    exp_q(i, c, 3)
                    ek_high(i)

            def turn_q(g):
                for j in range(NB):
                    act.wait_ge(s["eqT_ps"], NB * g + j + 1)
                    copy(eqT(g)[:, j, :], ps[:, BB + j, :], "eqT_ok")

            def normalise_y(g):
                act.wait_ge(s["y_norm"], g + 1)
                for t in range(NT):
                    y_t = y[g % NC][:, t, :]
                    act.activation(y_t, y_t, ACT.Identity, bias=yst[g % 2]["shift"][:, t:t + 1],
                                   scale=yst[g % 2]["r"][:, t:t + 1]).then_inc(s["yn_ok"], 1)

            def scale_shift(b, g):
                act.wait_ge(s["ab_step"], 3 * B)
                for f in range(NB):
                    act.wait_ge(s["ynT_ps"], NB * g + f + 1)
                    act.activation(u[f], ps[:, BB + f, :], ACT.Identity, bias=ab[:, b, 1, f:f + 1],
                                   scale=ab[:, b, 0, f:f + 1]).then_inc(s["u_ok"], 1)
                for f in range(NB):
                    act.wait_ge(s["u_ok"], NB * g + f + 1)
                    if g:
                        act.wait_ge(s["h_lo_ok"], NB * (g - 1) + f + 1)
                    act.activation(th[f], u[f], ACT.Tanh, scale=0.5).then_inc(s["th_ok"], 1)

            def h_high(g):
                for f in range(NB):
                    act.wait_ge(s["h_ok"], NB * g + f + 1)
                    copy(hT[g % 2][0][:, f, :], th[f], "h_hi_ok")

            act.wait_ge(s["ones_ok"], 1)
            act.activation(alpha[:], ones[:, 0:NB], ACT.Tanh).then_inc(s["table_ok"], 1)
            act.wait_ge(s["cols_ok"], 1)
            act.wait_ge(s["wk_in"], 16)
            for f in range(NB):
                copy(wk_hi[:, f, :], wk_raw[:, f, :], "wk_hi_ok", ln_weight(f))
            normalise_x(0)
            zT_high(0, BB)
            act.wait_ge(s["lnb_wq_step"], NB)
            for f in range(NB):
                copy(wq_raw[:, f, :], wq_raw[:, f, :], "wq_sc_ok", ln_weight(f))
            act.wait_ge(s["bk_ok"], 1)
            pen_with_bias(0, 0)
            pen_with_bias(0, 1)
            for f in range(NB):
                act.wait_ge(s["wq_sc_ok"], f + 1)
                copy(wq_hi[:, f, :], wq_raw[:, f, :], "wq_hi_ok")

            for b in range(B):
                i0 = b * NC
                if b:
                    act.wait_ge(s["h_lo_ok"], NB * i0)
                    pen_with_bias(i0, 0)
                    pen_with_bias(i0, 1)
                    act.wait_ge(s["o_ps"], NT * i0)
                phase1(i0, 0, True, False)
                if b == 0:
                    act.activation(semb_t[:], cols[:, COND:ROWS], ACT.Tanh, scale=0.5).then_inc(s["sig_ok"], 1)
                with act.Fori(1, NC - 1) as c:
                    phase1(i0 + c, c, False, False)
                phase1(i0 + NC - 1, NC - 1, False, True)

                act.wait_ge(s["z_hi_ok"], NT * (i0 + NC))
                act.wait_ge(s["z_lo_ok"], NT * (i0 + NC))
                turn_q(i0)
                if b == 0:
                    act.wait_ge(s["wo_in"], 16)
                    for f in range(NB):
                        copy(wo_hi[:, f, :], wo_raw[:, f, :], "wo_hi_ok", 0.5)
                    act.wait_ge(s["lnb_wv_step"], NB)
                    for f in range(NB):
                        copy(wv_sc[:, f, :], wv_raw[:, f, :], "wv_ok", ln_weight(f))
                act.wait_ge(s["wo_lo_ok"], NB)
                if b:
                    for t in range(NT):
                        act.wait_ge(stored[t], 16 * i0)
                for f in range(NB):
                    act.wait_ge(s["gT_ps"], NB * b + f + 1)
                    copy(gT[:, f, :], ps[:, BB + f, :], "gT_ok")
                exp_q(i0 + NC - 1, NC - 1, 2)
                exp_q(i0 + NC - 1, NC - 1, 3)
                if b == 0:
                    act.wait_ge(s["y_ps"], NT * (i0 + 1))
                turn_q(i0 + 1)
                normalise_y(i0)
                act.wait_ge(s["y_ps"], NT * (i0 + 2))
                turn_q(i0 + 2)
                scale_shift(b, i0)
                normalise_y(i0 + 1)
                h_high(i0)
                for g in range(i0 + 1, i0 + NC):
                    scale_shift(b, g)
                    if g + 1 < i0 + NC:
                        h_high(g)
                        normalise_y(g + 1)
                        if g == i0 + 1:
                            turn_q(i0 + 3)
                    else:
                        if b + 1 < B:
                            act.wait_ge(s["y_ps"], NT * (i0 + NC))
                            normalise_x(i0 + NC)
                        h_high(g)
                if b + 1 < B:
                    zT_high(i0 + NC, A)

        @block.gpsimd
        def _(pool):
            pool.memset(ident[:], 0.0).then_inc(s["ident0"], 1)
            pool.wait_ge(s["ident0"], 1)
            pool.affine_select(out=ident[:], in_=ident[:], compare_op=ALU.not_equal, fill=1.0, base=0,
                               pattern=[[-1, P]], channel_multiplier=1).then_inc(s["ident_ok"], 1)
            pool.wait_ge(s["bias_ps"], 1)
            pool.wait_ge(s["wk_lo_ok"], NB)
            pool.memset(g_acc[:], 0.0).then_inc(s["g_zero"], 1)
            for f in range(NB):
                pool.wait_ge(s["wq_hi_ok"], f + 1)
                pool.tensor_tensor(wq_lo[:, f, :], wq_raw[:, f, :], wq_hi[:, f, :].bitcast(F32),
                                   ALU.subtract).then_inc(s["wq_lo_ok"], 1)
            pool.wait_ge(s["bias_in"], 48)
            for b in range(B):
                if b:
                    pool.wait_ge(s["embT_ps"], 1)
                    pool.memset(g_acc[:], 0.0).then_inc(s["g_zero"], 1)
                with pool.Fori(b * NC, b * NC + NC) as i:
                    for t in range(NT):
                        pool.wait_ge(s["z_hi_ok"], NT * i + t + 1)
                        pool.tensor_tensor(z_lo[:, t, :], z[:, t, :], z_hi[:, t, :].bitcast(F32),
                                           ALU.subtract).then_inc(s["z_lo_ok"], 1)
                with pool.Fori(b * (NC // 2), b * (NC // 2) + NC // 2) as pair:
                    for k in range(2):
                        g = 2 * pair + k
                        for f in range(NB):
                            pool.wait_ge(s["h_hi_ok"], NB * g + f + 1)
                            pool.tensor_tensor(hT[k][1][:, f, :], th[f], hT[k][0][:, f, :].bitcast(F32),
                                               ALU.subtract).then_inc(s["h_lo_ok"], 1)
                        for t in range(NT):
                            pool.wait_ge(res_in[t], 16 * g + 16)
                            pool.tensor_tensor(res[:, t, :], res[:, t, :], bo_all[:], ALU.add).then_inc(s["res_b"], 1)

        @block.vector
        def _(dve):
            def carry():
                dve.memset(go[:], 0.0)

            def tile_stats(src, st, t, step):
                dve.bn_stats(st["raw"][:, t, :], src[:, t, :]).then_inc(s[step], 1)

            def finish_stats(st, step, base, done, between=lambda k: None):
                n = NT

                def link(ins):
                    nonlocal n
                    n += 1
                    ins.then_inc(s[step], 1)

                def here():
                    between(n - 2 * NT)
                    dve.wait_ge(s[step], base + n)

                dve.wait_ge(s[step], base + NT)
                carry()
                for t in range(NT):
                    link(dve.bn_aggr(st["mv"][:, t, :], st["raw"][:, t, :]))
                here()
                link(dve.tensor_scalar(st["v"][:], st["mv"][:, :, 1], EPS, None, ALU.add))
                here()
                link(dve.tensor_scalar(st["bits"][:], st["v"][:].bitcast(U32), 1, None, ALU.logical_shift_right))
                here()
                link(dve.tensor_scalar(st["y"][:], st["bits"][:], -1.0, float(RSQRT_SEED), ALU.mult, ALU.add))
                root = st["y"][:].bitcast(F32)
                for k in range(3):
                    here()
                    link(dve.scalar_tensor_tensor(out=st["a"][:], in0=root, scalar=-0.5, in1=root, op0=ALU.mult, op1=ALU.mult))
                    here()
                    link(dve.tensor_tensor(st["b"][:], st["a"][:], st["v"][:], ALU.mult))
                    here()
                    link(dve.scalar_tensor_tensor(out=st["r"][:], in0=st["b"][:], scalar=1.5, in1=root, op0=ALU.add, op1=ALU.mult))
                    root = st["r"][:]
                here()
                dve.scalar_tensor_tensor(out=st["shift"][:], in0=st["mv"][:, :, 0], scalar=-1.0, in1=root,
                                         op0=ALU.mult, op1=ALU.mult).then_inc(s[done], 1)
                assert n == STAT_STEPS, n

            def x_stats(i):
                if not isinstance(i, int) or i:
                    dve.wait_ge(s["x_ok"], 16 * i + 16)
                for t in range(NT):
                    if isinstance(i, int) and i == 0:
                        dve.wait_ge(s[("x0_ok", "x_ok")[t * 2 // NT]], 16)
                    tile_stats(x_in, xst, t, "xstat")
                finish_stats(xst, "xstat", STAT_STEPS * i, "x_norm")

            def penalty(i):
                dve.wait_ge(s["mask_ok"], 16 * i + 16)
                if not isinstance(i, int) or i:
                    dve.wait_ge(s["penb_ok"], NB * i)
                dve.tensor_scalar(pen[:], mrow[:], 1.0, MASK_PENALTY, ALU.subtract, ALU.mult).then_inc(s["pen_ok"], 1)

            def zT_low(i, bank):
                for f in range(NB):
                    dve.wait_ge(s["zT_hi_ok"], NB * i + f + 1)
                    dve.tensor_tensor(zT_lo[:, f, :], ps[:, bank + f, :], zT_hi[:, f, :].bitcast(F32),
                                      ALU.subtract).then_inc(s["zT_lo_ok"], 1)

            def k_phase(i, between=lambda j: None, free=lambda j: None):
                def masked(j):
                    free(j)
                    dve.wait_ge(s["k_exp"], NB * i + j + 1)
                    dve.scalar_tensor_tensor(out=ekTm[:, j, :], in0=ekT[:, j % 2, :], scalar=1.0, in1=mrow[:],
                                             op0=ALU.mult, op1=ALU.mult,
                                             accum_out=zs_new[:, 1, j:j + 1]).then_inc(s["k_masked"], 1)

                for j in range(NB):
                    n = NB * i + j + 1
                    dve.wait_ge(s["penb_ok"], n)
                    if j >= 2:
                        dve.wait_ge(s["k_exp"], NB * i + j - 1)
                    dve.wait_ge(s["k_ps"], n)
                    carry()
                    dve.tensor_tensor_reduce(kT[:, j % 2, :], ps[:, BB + j, :], pen_bias[:, j % 2, :], 1.0,
                                             kmax[:, j:j + 1], ALU.add, ALU.max,
                                             kmax_new[:, j:j + 1]).then_inc(s["k_max"], 1)
                    if j:
                        masked(j - 1)
                    dve.wait_ge(s["k_max"], n)
                    dve.tensor_scalar(nmax[:, j:j + 1], kmax_new[:, j:j + 1], -1.0, None, ALU.mult).then_inc(s["k_nmax"], 1)
                    between(j)
                masked(NB - 1)

            def g_phase(i):
                for j in range(NB):
                    dve.wait_ge(s["k_alpha"], i + 1)
                    dve.wait_ge(s["g_ps"], NB * i + j + 1)
                    dve.scalar_tensor_tensor(out=g_acc[:, j, :], in0=g_acc[:, j, :], scalar=alpha[:, j:j + 1],
                                             in1=ps[:, A + j, :], op0=ALU.mult, op1=ALU.add).then_inc(s["g_ok"], 1)

            def q_tile(i, t, bank):
                n = NT * i + t + 1
                dve.wait_ge(s["q_ps"], n)
                if t >= 2:
                    dve.wait_ge(s["q_exp"], NT * i + t - 1)
                dve.tensor_tensor(qs[:, t % 2, :], ps[:, bank, :], bq_all[:], ALU.add).then_inc(s["q_sum"], 1)
                q_heads = qs[:, t % 2, :].rearrange("p (h d) -> p h d", h=H)
                dve.wait_ge(s["q_sum"], n)
                dve.tensor_reduce(qmax[:, t % 2, :], q_heads, AX_X, ALU.max).then_inc(s["q_max"], 1)
                dve.wait_ge(s["q_max"], n)
                dve.tensor_tensor(q_heads, q_heads, qmax[:, t % 2, :].unsqueeze(2).broadcast_to([P, H, DH]),
                                  ALU.subtract).then_inc(s["q_shift"], 1)

            def ek_low(i):
                for t in range(NT):
                    dve.wait_ge(s["ek_hi_ok"], NT * i + t + 1)
                    dve.tensor_tensor(ek_lo[:, t, :], ps[:, A + t, :], ek_hi[:, t, :].bitcast(F32),
                                      ALU.subtract).then_inc(s["ek_lo_ok"], 1)

            def after_k(i, first, left):
                if not first:
                    g_phase(i - 1)
                dve.wait_ge(s["k_max"], NB * i + NB)
                dve.tensor_tensor(dmax[:], kmax[:], kmax_new[:], ALU.subtract).then_inc(s["k_shift"], 1)
                dve.wait_ge(s["k_shift"], i + 1)
                dve.tensor_copy(kmax[:], kmax_new[:]).then_inc(s["k_saved"], 1)
                q_tile(i, 0, BB)
                dve.wait_ge(s["k_alpha"], i + 1)
                dve.wait_ge(s["k_masked"], NB * i + NB)
                dve.tensor_tensor(zs[:], zs[:], alpha[:].unsqueeze(1).broadcast_to([P, 2, NB]), ALU.mult).then_inc(s["zs_step"], 1)
                dve.wait_ge(s["zs_step"], 2 * i + 1)
                dve.tensor_tensor(zs[:], zs[:], zs_new[:], ALU.add).then_inc(s["zs_step"], 1)
                q_tile(i, 1, BB + 1)
                if left:
                    q_tile(i, 2, BB + 2)
                    q_tile(i, 3, BB + 3)
                    zT_low(i + 1, BB)
                ek_low(i)
                if left:
                    penalty(i + 1)
                if left > 1 and not first:
                    x_stats(i + 2)

            def reset(b):
                if b:
                    dve.wait_ge(s["k_saved"], NC * b)
                    dve.wait_ge(s["att_step"], 6 * b)
                dve.memset(kmax[:], -LEAST)
                dve.memset(zs[:], 0.0).then_inc(s["reset_ok"], 1)
                dve.wait_ge(s["reset_ok"], b + 1)

            def condition_scale():
                dve.wait_ge(s["embT_ps"], 1)
                for b in range(B):
                    dve.tensor_tensor(emb_cols[:, b, :], ps[:, BB + 3, 0:2 * B * NB].rearrange("p (c b) -> p b c", b=B)[:, b, :],
                                      cols[:, BEMB:BEMB + 2 * NB], ALU.add).then_inc(s["embc_ok"], 1)
                dve.wait_ge(s["embc_ok"], B)
                for b in range(B):
                    for k, w in ((0, LN2W), (1, LN2B)):
                        dve.scalar_tensor_tensor(out=ab[:, b, k, :], in0=emb_cols[:, b, 0:NB], scalar=1.0,
                                                 in1=cols[:, w:w + NB], op0=ALU.add, op1=ALU.mult).then_inc(s["ab_step"], 1)
                    dve.wait_ge(s["ab_step"], 3 * b + 2)
                    dve.tensor_tensor(ab[:, b, 1, :], ab[:, b, 1, :], emb_cols[:, b, NB:2 * NB],
                                      ALU.add).then_inc(s["ab_step"], 1)

            def att_blocks(b):
                dve.wait_ge(s["zs_step"], 2 * NC * (b + 1))
                dve.reciprocal(rz[:], zs[:, 0, :]).then_inc(s["rz_ok"], 1)
                rows = [slice(DH * h, DH * h + DH) for h in range(2)]
                part = [pen[r, 0:NB * DH].rearrange("p (q d) -> p q d", q=NB) for r in rows]

                def of_head(t, h):
                    return t[rows[h], :].rearrange("p (q h d) -> p q h d", q=NB, h=2)[:, :, h, :]

                for h, r in enumerate(rows):
                    dve.tensor_tensor(part[h], of_head(bv_all, h), zs[r, 1, :].unsqueeze(2).broadcast_to([DH, NB, DH]),
                                      ALU.mult).then_inc(s["att_step"], 1)
                dve.wait_ge(s["rz_ok"], b + 1)
                dve.wait_ge(s["att_ps"], b + 1)
                dve.wait_ge(s["att_step"], 6 * b + 2)
                for h in range(2):
                    dve.tensor_tensor(part[h], part[h], of_head(ps[:, A + 1, :], h), ALU.add).then_inc(s["att_step"], 1)
                dve.wait_ge(s["att_step"], 6 * b + 4)
                for h, r in enumerate(rows):
                    dve.tensor_tensor(att[r, :, DH * h:DH * h + DH], part[h],
                                      rz[r, :].unsqueeze(2).broadcast_to([DH, NB, DH]), ALU.mult).then_inc(s["att_step"], 1)

            def y_tile(g, t):
                n = NT * g + t + 1
                tile = ps[:, A + 2 * (t % 2):A + 2 * (t % 2) + 2, :].rearrange("p k (q c) -> p (k q) c", c=YS)
                rec_t = rec[:, t % 2, :].rearrange("p (q h) -> p q h", h=2)
                dve.wait_ge(s["y_ps"], n)
                if n > 2:
                    dve.wait_ge(s["y_ok"], n - 2)
                dve.reciprocal(rec_t, tile[:, :, P:YW]).then_inc(s["y_rec"], 1)
                dve.wait_ge(s["y_rec"], n)
                dve.tensor_tensor(y[g % NC][:, t, :].rearrange("p (q h d) -> p q h d", q=NB, h=2),
                                  tile[:, :, 0:P].rearrange("p q (h d) -> p q h d", h=2),
                                  rec_t.unsqueeze(3).broadcast_to([P, NB, 2, DH]), ALU.mult).then_inc(s["y_ok"], 1)

            def y_tile_stats(g, t):
                dve.wait_ge(s["y_ok"], NT * g + t + 1)
                tile_stats(y[g % NC], yst[g % 2], t, "ystat")

            def y_finish(g, between=lambda k: None):
                finish_stats(yst[g % 2], "ystat", STAT_STEPS * g, "y_norm", between)

            def y_with_stats(g):
                for t in range(NT + 1):
                    if t < NT:
                        y_tile(g, t)
                    if t:
                        y_tile_stats(g, t - 1)

            def every(steps, do):
                return lambda k: do(k // steps) if k % steps == 0 and k // steps < 4 else None

            def silu_block(g, f):
                dve.wait_ge(s["th_ok"], NB * g + f + 1)
                dve.scalar_tensor_tensor(out=th[f], in0=th[f], scalar=1.0, in1=u[f],
                                         op0=ALU.add, op1=ALU.mult).then_inc(s["h_ok"], 1)

            def out_tile(g, t):
                dve.wait_ge(s["o_ps"], NT * g + t + 1)
                dve.wait_ge(s["res_b"], NT * g + t + 1)
                dve.tensor_tensor(res[:, t, :], ps[:, BB + t, :], res[:, t, :], ALU.add).then_inc(s["o_ok"], 1)

            dve.memset(ones[:], 1.0).then_inc(s["ones_ok"], 1)
            dve.memset(att[:], 0.0).then_inc(s["att0"], 1)
            dve.wait_ge(s["att0"], 1)
            dve.memset(att[0:DH, :, P:P + 1], 1.0).then_inc(s["att0"], 1)
            dve.memset(att[DH:P, :, P + 1:P + 2], 1.0).then_inc(s["att0"], 1)
            dve.wait_ge(s["vec_ps"], 1)
            dve.tensor_copy(cols[:, 0:FIRST], ps[:, 0, 0:FIRST]).then_inc(s["cols_ok"], 1)
            dve.wait_ge(s["cols_ok"], 1)
            dve.wait_ge(s["ones_ok"], 1)
            for f in range(NB):
                dve.tensor_scalar(lnb_wide[:, f, :], ones[:], cols[:, LNB + f:LNB + f + 1], None,
                                  ALU.mult).then_inc(s["lnb_ok"], 1)
            x_stats(0)

            def weighted_by_lnb(to, raw, step):
                dve.tensor_scalar(to, raw[:, 0, :], cols[:, LNB:LNB + 1], None, ALU.mult).then_inc(s[step], 1)
                for f in range(1, NB):
                    dve.wait_ge(s[step], f)
                    dve.scalar_tensor_tensor(out=to, in0=raw[:, f, :], scalar=cols[:, LNB + f:LNB + f + 1], in1=to,
                                             op0=ALU.mult, op1=ALU.add).then_inc(s[step], 1)

            for f in range(NB):
                dve.wait_ge(s["wk_hi_ok"], f + 1)
                dve.scalar_tensor_tensor(out=wk_lo[:, f, :], in0=wk_raw[:, f, :], scalar=cols[:, LNW + f:LNW + f + 1],
                                         in1=wk_hi[:, f, :].bitcast(F32), op0=ALU.mult,
                                         op1=ALU.subtract).then_inc(s["wk_lo_ok"], 1)
            dve.wait_ge(s["wq_in"], 16)
            weighted_by_lnb(lnb_wq, wq_raw, "lnb_wq_step")
            dve.wait_ge(s["bias_ps"], 1)
            dve.tensor_copy(bk_rows, ps[:, 1, :]).then_inc(s["bk_row_ok"], 1)
            zT_low(0, BB)
            dve.wait_ge(s["vec_ps"], 2)
            dve.tensor_copy(cols[:, FIRST:ROWS], ps[:, 0, 0:ROWS - FIRST]).then_inc(s["cols_ok"], 1)
            dve.wait_ge(s["cols_ok"], 2)
            dve.wait_ge(s["bk_ps"], 1)
            dve.tensor_tensor(cols[:, BK:BK + NB], cols[:, BK:BK + NB],
                              ps[:, 3, :].rearrange("p (j c) -> p j c", j=NB)[:, :, 0], ALU.add).then_inc(s["bk_ok"], 1)
            penalty(0)
            reset(0)
            dve.wait_ge(s["bias_in"], 48)
            dve.wait_ge(s["bias_ps"], 2)
            dve.tensor_tensor(bq_all[:], bq_all[:], ps[:, 2, :], ALU.add).then_inc(s["bq_ok"], 1)
            dve.wait_ge(s["bq_ok"], 1)

            for b in range(B):
                i0 = b * NC
                if b == 0:
                    dve.wait_ge(s["x_ok"], 32)


                    def stats_of_next(j):
                        if j < 2:
                            for t in (2 * j, 2 * j + 1):
                                tile_stats(x_in, xst, t, "xstat")
                        elif j == 3:
                            finish_stats(xst, "xstat", STAT_STEPS, "x_norm")

                    k_phase(i0, stats_of_next, lambda j: dve.wait_ge(s["wq_lo_ok"], j + 1))
                else:
                    k_phase(i0)
                after_k(i0, True, 2)
                x_stats(i0 + 2)
                if b == 0:
                    dve.wait_ge(s["sig_ok"], 1)
                    dve.scalar_tensor_tensor(out=semb_t[:], in0=semb_t[:], scalar=1.0, in1=cols[:, COND:ROWS],
                                             op0=ALU.add, op1=ALU.mult).then_inc(s["semb_step"], 1)
                    dve.wait_ge(s["semb_step"], 1)
                    dve.tensor_scalar(semb[:], semb_t[:].rearrange("p (b t) -> p t b", b=B), 0.5, None,
                                      ALU.mult).then_inc(s["semb_ok"], 1)
                dve.wait_ge(s["g_zero"], b + 1)
                with dve.Fori(1, NC - 2) as c:
                    k_phase(i0 + c)
                    after_k(i0 + c, False, 2)
                for left in (1, 0):
                    k_phase(i0 + NC - 1 - left)
                    after_k(i0 + NC - 1 - left, False, left)
                if b == 0:
                    for f in range(NB):
                        dve.wait_ge(s["wo_hi_ok"], f + 1)
                        dve.scalar_tensor_tensor(out=wo_lo[:, f, :], in0=wo_raw[:, f, :], scalar=0.5,
                                                 in1=wo_hi[:, f, :].bitcast(F32), op0=ALU.mult,
                                                 op1=ALU.subtract).then_inc(s["wo_lo_ok"], 1)
                    dve.wait_ge(s["wo_lo_ok"], NB)
                    dve.wait_ge(s["wv_in"], 16)
                    weighted_by_lnb(lnb_wv, wv_raw, "lnb_wv_step")
                g_phase(i0 + NC - 1)
                if b == 0:
                    dve.wait_ge(s["bias_ps"], 3)
                    dve.tensor_tensor(bv_all[:], bv_all[:], ps[:, A + 2, :], ALU.add).then_inc(s["bv_ok"], 1)
                    dve.wait_ge(s["bv_ok"], 1)
                q_tile(i0 + NC - 1, 2, BB + 3)
                if b == 0:
                    dve.wait_ge(s["emb_ps"], 1)
                    dve.tensor_copy(emb_rows[:, 0:D], ps[0:B, A, :]).then_inc(s["emb_ok"], 1)
                q_tile(i0 + NC - 1, 3, A + 3)
                att_blocks(b)

                y_with_stats(i0)
                y_finish(i0)
                if b == 0:
                    for t in range(2):
                        y_tile(i0 + 1, t)
                    for t in range(2):
                        y_tile_stats(i0 + 1, t)
                    dve.wait_ge(s["emb_ps"], 2)
                    dve.tensor_copy(emb_rows[:, D:2 * D], ps[0:B, BB, :]).then_inc(s["emb_ok"], 1)
                    for t in range(2, NT):
                        y_tile(i0 + 1, t)
                    condition_scale()
                    for t in range(2, NT):
                        y_tile_stats(i0 + 1, t)
                else:
                    y_with_stats(i0 + 1)
                y_finish(i0 + 1)
                y_tile(i0 + 2, 0)
                y_tile(i0 + 2, 1)
                for t in range(NT):
                    silu_block(i0, t)
                y_tile(i0 + 2, 2)
                y_tile(i0 + 2, 3)
                for t in range(NT):
                    y_tile_stats(i0 + 2, t)
                y_finish(i0 + 2, every(3, lambda t: silu_block(i0 + 1, t)))
                for t in range(NT):
                    out_tile(i0, t)
                y_with_stats(i0 + 3)
                y_finish(i0 + 3, every(3, lambda t: silu_block(i0 + 2, t)))
                for t in range(NT):
                    out_tile(i0 + 1, t)
                if b + 1 < B:
                    x_stats(i0 + NC)
                for t in range(NT):
                    silu_block(i0 + 3, t)
                for t in range(NT):
                    out_tile(i0 + 2, t)
                if b + 1 < B:
                    penalty(i0 + NC)
                    zT_low(i0 + NC, A)
                    reset(b + 1)
                out_tile(i0 + 3, 0)
                out_tile(i0 + 3, 1)
                if b + 1 < B:
                    x_stats(i0 + NC + 1)
                out_tile(i0 + 3, 2)
                out_tile(i0 + 3, 3)

        @block.tensor
        def _(pe):
            def split_product(o, a, bb, start, stop):
                pe.matmul(o, a[0], bb[0], start=start, stop=False)
                pe.matmul(o, a[0], bb[1], start=False, stop=False)
                return pe.matmul(o, a[1], bb[0], start=False, stop=stop)

            def turn(o, i):
                return pe.transpose(o, i, ident[0:i.shape[0], 0:i.shape[0]])

            def turn_z(i, bank, free):
                for f in range(NB):
                    free(f)
                    for t in range(NT):
                        if f == 0:
                            pe.wait_ge(s["z_ok"], NT * i + t + 1)
                        last = turn(blk(ps[:, bank + f, :], t), blk(z[:, t, :], f))
                    last.then_inc(s["zT_ps"], 1)

            def products_k(i, free):
                for j in range(NB):
                    free(j)
                    for f in range(NB):
                        if j == 0:
                            pe.wait_ge(s["zT_lo_ok"], NB * i + f + 1)
                        last = split_product(ps[:, BB + j, :], (blk(wk_hi[:, f, :], j), blk(wk_lo[:, f, :], j)),
                                             (zT_hi[:, f, :], zT_lo[:, f, :]), f == 0, f == NB - 1)
                    last.then_inc(s["k_ps"], 1)

            def products_q(i, t, bank):
                for f in range(NB):
                    last = split_product(ps[:, bank, :], (blk(zT_hi[:, f, :], t), blk(zT_lo[:, f, :], t)),
                                         (wq_hi[:, f, :], wq_lo[:, f, :]), f == 0, f == NB - 1)
                last.then_inc(s["q_ps"], 1)

            def products_all_q(i):
                for t in range(NT):
                    pe.wait_ge(s["k_max"], NB * i + t + 1)
                    products_q(i, t, BB + t)

            def turn_k(i):
                pe.wait_ge(s["k_masked"], NB * i + NB)
                for t in range(NT):
                    for j in range(NB):
                        last = turn(blk(ps[:, A + t, :], j), blk(ekTm[:, j, :], t))
                    last.then_inc(s["ek_ps"], 1)

            def products_g(i):
                for t in range(NT):
                    pe.wait_ge(s["z_lo_ok"], NT * i + t + 1)
                    for j in range(NB):
                        if t == 0:
                            pe.wait_ge(s["ek_lo_ok"], NT * i + j + 1)
                        last = split_product(ps[:, A + j, :], (blk(ek_hi[:, t, :], j), blk(ek_lo[:, t, :], j)),
                                             (z_hi[:, t, :], z_lo[:, t, :]), t == 0, t == NT - 1)
                        if t == NT - 1:
                            last.then_inc(s["g_ps"], 1)

            def turn_q(g, free):
                pe.wait_ge(s["q_exp"], NT * g + NT)
                for j in range(NB):
                    free(j)
                    for t in range(NT):
                        last = turn(blk(ps[:, BB + j, :], t), blk(eq[:, (g % NC) * NT + t, :], j))
                    last.then_inc(s["eqT_ps"], 1)

            def products_y(g, tiles=range(NT)):
                pe.wait_ge(s["eqT_ok"], NB * g + NB)
                for t in tiles:
                    if NT * g + t > 1:
                        pe.wait_ge(s["y_ok"], NT * g + t - 1)
                    for q in range(NB):
                        bank, at = A + 2 * (t % 2) + q // 2, (q % 2) * YS
                        last = pe.matmul(ps[:, bank, at:at + YW], blk(eqT(g)[:, q, :], t), att[:, q, :], start=True, stop=True)
                    last.then_inc(s["y_ps"], 1)

            def turn_y(g, free):
                for f in range(NB):
                    free(f)
                    for t in range(NT):
                        if f == 0:
                            pe.wait_ge(s["yn_ok"], NT * g + t + 1)
                        last = turn(blk(ps[:, BB + f, :], t), blk(y[g % NC][:, t, :], f))
                    last.then_inc(s["ynT_ps"], 1)

            def products_out(g, free):
                for t in range(NT):
                    free(t)
                    for f in range(NB):
                        if t == 0:
                            pe.wait_ge(s["h_lo_ok"], NB * g + f + 1)
                        hi, lo = hT[g % 2]
                        last = split_product(ps[:, BB + t, :], (blk(hi[:, f, :], t), blk(lo[:, f, :], t)),
                                             (wo_hi[:, f, :], wo_lo[:, f, :]), f == 0, f == NB - 1)
                    last.then_inc(s["o_ps"], 1)

            def condition(h, bank, tiles=range(NTE)):
                for t in tiles:
                    n = NTE * h + t
                    pe.wait_ge(wemb_in[n], 16)
                    last = pe.matmul(ps[0:B, bank, :], semb[:, t, :], wemb[n % NW], start=(t == 0), stop=(t == NTE - 1))
                if tiles[-1] == NTE - 1:
                    last.then_inc(s["emb_ps"], 1)

            def ready(name, n):
                return lambda k: pe.wait_ge(s[name], n + k)

            pe.wait_ge(s["ident_ok"], 1)
            pe.wait_ge(s["ln_in"], 2 * 16)
            turn(ps[:, 0, 0:FIRST], ln_rows).then_inc(s["vec_ps"], 1)
            pe.wait_ge(s["lnb_ok"], NB)
            pe.wait_ge(s["wk_in"], 16)
            for f in range(NB):
                last = pe.matmul(ps[:, 1, :], lnb_wide[:, f, :], wk_raw[:, f, :], start=(f == 0), stop=(f == NB - 1))
            last.then_inc(s["bias_ps"], 1)
            turn_z(0, BB, lambda f: None)
            pe.wait_ge(s["lnb_wq_step"], NB)
            pe.matmul(ps[:, 2, :], ones[:], lnb_wq, start=True, stop=True).then_inc(s["bias_ps"], 1)
            pe.wait_ge(s["bk_row_ok"], 1)
            for j in range(NB):
                last = turn(blk(ps[:, 3, :], j), blk(bk_rows, j))
            last.then_inc(s["bk_ps"], 1)
            pe.wait_ge(s["vec_in"], 5 * 16)
            pe.wait_ge(s["cols_ok"], 1)
            turn(ps[:, 0, 0:ROWS - FIRST], vec_rows[:]).then_inc(s["vec_ps"], 1)
            pe.wait_ge(s["wk_lo_ok"], NB)

            for b in range(B):
                i0 = b * NC
                products_k(i0, ready("o_ok", NT * (i0 - 1) + 1) if b else lambda j: None)
                if b == 0:
                    pe.wait_ge(s["wq_lo_ok"], NB)
                products_all_q(i0)
                turn_z(i0 + 1, BB, ready("q_sum", NT * i0 + 1))
                if b == 0:
                    pe.wait_ge(s["bq_ok"], 1)
                turn_k(i0)
                with pe.Fori(1, NC - 1) as c:
                    i = i0 + c
                    products_k(i, lambda j: None)
                    products_g(i - 1)
                    products_all_q(i)
                    pe.wait_ge(s["g_ok"], NB * i)
                    turn_z(i + 1, BB, ready("q_sum", NT * i + 1))
                    turn_k(i)
                i = i0 + NC - 1
                products_k(i, lambda j: None)
                products_g(i - 1)
                for t in range(2):
                    pe.wait_ge(s["k_max"], NB * i + t + 1)
                    products_q(i, t, BB + t)
                pe.wait_ge(s["g_ok"], NB * i)
                turn_k(i)
                pe.wait_ge(s["k_max"], NB * i + NB)
                turn_q(i0, lambda j: pe.wait_ge(s["q_sum"], NT * i + j + 1) if j < 2 else None)
                products_g(i)
                pe.wait_ge(s["eqT_ok"], NB * i0 + NB)
                products_q(i, 2, BB + 3)

                pe.wait_ge(s["g_ok"], NB * i + NB)
                if b == 0:
                    pe.wait_ge(s["lnb_wv_step"], NB)
                    pe.matmul(ps[:, A + 2, :], ones[:], lnb_wv, start=True, stop=True).then_inc(s["bias_ps"], 1)
                for f in range(NB):
                    if f == NB - 1:
                        pe.wait_ge(s["q_sum"], NT * i + 3)
                    for j in range(NB):
                        last = turn(blk(ps[:, BB + f, :], j), blk(g_acc[:, j, :], f))
                    last.then_inc(s["gT_ps"], 1)
                if b == 0:
                    pe.wait_ge(s["semb_ok"], 1)
                    condition(0, A)
                    pe.wait_ge(s["wv_ok"], NB)
                products_q(i, 3, A + 3)
                pe.wait_ge(s["gT_ok"], NB * b + NB)
                for q in range(NB):
                    for f in range(NB):
                        last = pe.matmul(blk(ps[:, A + 1, :], q), blk(gT[:, f, :], q), blk(wv_sc[:, f, :], q),
                                         start=(f == 0), stop=(f == NB - 1))
                last.then_inc(s["att_ps"], 1)
                turn_q(i0 + 1, lambda j: None)
                if b == 0:
                    pe.wait_ge(s["emb_ok"], 1)
                pe.wait_ge(s["bv_ok"], 1)
                pe.wait_ge(s["q_sum"], NT * i + NT)
                pe.wait_ge(s["att_step"], 6 * b + 6)
                products_y(i0)
                if b == 0:
                    pe.wait_ge(s["eqT_ok"], NB * (i0 + 1) + 1)
                    condition(1, BB, range(NTE // 2))
                products_y(i0 + 1, range(0, 2))
                if b == 0:
                    condition(1, BB, range(NTE // 2, NTE))
                    products_y(i0 + 1, range(2, NT))
                    pe.wait_ge(s["emb_ok"], 2)
                    for k in range(2 * NB):
                        last = turn(ps[:, BB + 3, B * k:B * k + B], blk(emb_rows, k))
                    last.then_inc(s["embT_ps"], 1)
                    turn_q(i0 + 2, lambda j: pe.wait_ge(s["embc_ok"], B) if j == 3 else None)
                else:
                    turn_q(i0 + 2, lambda j: None)
                    products_y(i0 + 1, range(2, NT))
                turn_y(i0, ready("eqT_ok", NB * (i0 + 2) + 1))
                products_y(i0 + 2)
                turn_y(i0 + 1, ready("u_ok", NB * i0 + 1))
                products_out(i0, ready("u_ok", NB * (i0 + 1) + 1))
                turn_q(i0 + 3, ready("o_ok", NT * i0 + 1))
                turn_y(i0 + 2, ready("eqT_ok", NB * (i0 + 3) + 1))
                products_y(i0 + 3)
                products_out(i0 + 1, ready("u_ok", NB * (i0 + 2) + 1))
                turn_y(i0 + 3, ready("o_ok", NT * (i0 + 1) + 1))
                products_out(i0 + 2, ready("u_ok", NB * (i0 + 3) + 1))
                if b + 1 < B:
                    turn_z(i0 + NC, A, lambda f: None)
                products_out(i0 + NC - 1, ready("o_ok", NT * (i0 + NC - 2) + 1))


_INS = ["x", "cond_2048", "mask_BxSx1_fk1"] + ["L0_cond_" + n for n in (
    "ln_w", "ln_b", "Wq", "bq", "Wk", "bk", "Wv", "bv", "W_emb", "b_emb", "ln2_w", "ln2_b", "W_out", "b_out")]


def kernel(**inputs):
    import numpy as _np
    import concourse.bacc as _bacc
    from concourse import mybir as _mybir
    from concourse.bass_utils import run_bass_kernel_spmd as _run

    nc = _bacc.Bacc("TRN2", target_bir_lowering=False, num_devices=1)
    arrays, args = {}, []
    for name in _INS:
        a = _np.ascontiguousarray(inputs[name])
        arrays[f"in_{name}_dram"] = a
        args.append(nc.dram_tensor(f"in_{name}_dram", a.shape, _mybir.dt.from_np(a.dtype), kind="ExternalInput").ap())
    shape = _np.shape(inputs["x"])
    args.append(nc.dram_tensor("out_dram", shape, _mybir.dt.float32, kind="ExternalOutput").ap())
    cond_linear_attention(nc, *args)
    r = _run(nc, [arrays], core_ids=[0])
    return r.results[0]["out_dram"]
```
